# Optimizing a Trainium2 kernel written in Bass

```python
import numpy as np
import jax
import jax.numpy as jnp

def _softmax(x, axis=-1):
    return jax.nn.softmax(x, axis=axis)

def _gelu(x):
    return jax.nn.gelu(x, approximate=True)

def _silu(x):
    return jax.nn.silu(x)

def _sigmoid(x):
    return jax.nn.sigmoid(x)

def _layernorm(x, axis=-1, eps=1e-05):
    m = jnp.mean(x, axis=axis, keepdims=True)
    v = jnp.var(x, axis=axis, keepdims=True)
    return (x - m) / jnp.sqrt(v + eps)

def _scatter_add(tgt, idx, src, axis=0):
    return tgt.at[idx].add(src)

def _segment_sum(src, seg, n):
    return jax.ops.segment_sum(src, seg, n)
kernel_name = 'mk_adj_resnorm_d1_adj_r2_c54ca4'

def setup_inputs(seed: int=0):
    np.random.seed(seed)
    _w = jnp.asarray

    def _rec_inputs():
        import jax
        import jax.numpy as jnp
        _gk = jax.random.key(seed)
        x = -0.0002928 + 1 * jax.random.normal(jax.random.fold_in(_gk, 1), (16, 512, 256), jnp.float32)
        _w = (1.0 + jnp.arange(512, dtype=jnp.float32)) ** (-0.5)
        _w = _w / _w.mean()
        _pij = jnp.clip(0.0078125 * _w[:, None] * _w[None, :], 0.0, 1.0)
        _a = jax.random.uniform(jax.random.fold_in(_gk, 2), (16, 512, 512)) < _pij
        _a = jnp.logical_or(_a, jnp.swapaxes(_a, -1, -2))
        _a = jnp.logical_or(_a, jnp.eye(512, dtype=bool))
        _af = _a.astype(jnp.float32)
        _af = _af * jax.random.uniform(jax.random.fold_in(_gk, 3), (16, 512, 512), jnp.float32, 0.05, 1)
        adj = _af
        return (x, adj)
    x, adj = _rec_inputs()

    def _L0_gnn_setup():
        import jax, jax.numpy as jnp
        import numpy as np
        B, N, DIN, DOUT, K = (4, 1024, 256, 256, 3)
        key = jax.random.key(seed)
        ks = jax.random.split(key, 8)
        X = jax.random.normal(ks[0], (B, N, DIN), dtype=jnp.float32)
        A = jax.random.uniform(ks[1], (B, N, N), dtype=jnp.float32)
        Wv = jax.random.normal(ks[2], (DIN, DOUT), dtype=jnp.float32) * 0.02
        bv = jax.random.normal(ks[3], (DOUT,), dtype=jnp.float32) * 0.02
        aw = jax.random.normal(ks[4], (2 * DOUT, 1), dtype=jnp.float32) * 0.05
        ab = jax.random.normal(ks[5], (1,), dtype=jnp.float32) * 0.05
        Wk = jax.random.normal(ks[6], (K, DIN, DOUT), dtype=jnp.float32) * 0.02
        bk = jax.random.normal(ks[7], (K, DOUT), dtype=jnp.float32) * 0.02
        return {'X': X, 'A': A, 'Wv': Wv, 'bv': bv, 'aw': aw, 'ab': ab, 'Wk': Wk, 'bk': bk}
    _L0_gnn_all = _L0_gnn_setup()
    _L0_gnn_in = {k: v for k, v in _L0_gnn_all.items() if k in ('Wv', 'bv', 'aw', 'ab', 'Wk', 'bk')}
    del _L0_gnn_all
    return {'x': x, 'adj': adj, 'L0_gnn_Wv': _L0_gnn_in['Wv'], 'L0_gnn_bv': _L0_gnn_in['bv'], 'L0_gnn_aw': _L0_gnn_in['aw'], 'L0_gnn_ab': _L0_gnn_in['ab'], 'L0_gnn_Wk': _L0_gnn_in['Wk'], 'L0_gnn_bk': _L0_gnn_in['bk']}

def reference(x, adj, L0_gnn_Wv, L0_gnn_bv, L0_gnn_aw, L0_gnn_ab, L0_gnn_Wk, L0_gnn_bk):
    import jax
    import jax.numpy as jnp

    def _L0_gnn_ref(X, A, Wv, bv, aw, ab, Wk, bk):
        import jax, jax.numpy as jnp
        import numpy as np
        B, N, DIN, DOUT, K = (4, 1024, 256, 256, 3)
        d = Wv.shape[1]
        Xw = X @ Wv + bv
        sj = Xw @ aw[:d, 0]
        si = Xw @ aw[d:, 0]
        e = jax.nn.leaky_relu(sj[:, None, :] + si[:, :, None] + ab[0], negative_slope=0.2)
        alpha_matrix = A * jnp.exp(e)
        transition = alpha_matrix / (jnp.sum(alpha_matrix, axis=-1, keepdims=True) + 1e-12)
        H = jnp.zeros(X.shape[:-1] + (d,), dtype=X.dtype)
        Xk = X
        for k in range(Wk.shape[0]):
            H = H + Xk @ Wk[k] + bk[k]
            Xk = jnp.einsum('bij,bjd->bid', transition, Xk)
        return jax.nn.relu(H)
    x = _layernorm(x + _L0_gnn_ref(x, adj, L0_gnn_Wv, L0_gnn_bv, L0_gnn_aw, L0_gnn_ab, L0_gnn_Wk, L0_gnn_bk), axis=-1)
    return x

_drawn_inputs = setup_inputs


def setup_inputs(seed=0):
    import zlib

    import numpy as np

    out = dict(_drawn_inputs(seed))
    spreads = {}
    factors = {'L0_gnn_Wv': 3.424, 'L0_gnn_bv': 21.532, 'L0_gnn_aw': 3.482}
    for name, (base, spread) in spreads.items():
        noise = np.random.default_rng([zlib.crc32(name.encode()), seed]).standard_normal(out[name].shape)
        drawn = base * np.exp(spread * noise) if base else spread * noise
        out[name] = jnp.asarray(drawn.astype(out[name].dtype))
    for name, factor in factors.items():
        out[name] = (out[name] * factor).astype(out[name].dtype)
    return out
```

```python
from collections import namedtuple
from contextlib import ExitStack

from concourse import mybir

ALU = mybir.AluOpType
ACT = mybir.ActivationFunctionType
F32 = mybir.dt.float32
F32R = mybir.dt.float32r

P = 128
SLOPE = 0.2
SUM_EPS = 1e-12
VAR_EPS = 1e-5

Batch = namedtuple("Batch", "at pair slot")


def batch(number):
    return Batch(number, number // 2, number % 2)


def in_loop(i, ahead):
    return Batch(2 * i + ahead, i + ahead // 2, ahead % 2)


def after(engine, semaphore, count):
    if not isinstance(count, int) or count > 0:
        engine.wait_ge(semaphore, count)


def gnn_resnorm(nc, x, adj, Wv, bv, aw, ab, Wk, bk, out):
    B, N, D = x.shape
    HOPS = Wk.shape[0]
    NT = N // P
    DT = D // P
    WA = 2 * D
    WB = D + 4
    SJ, SJ_REST, SI = D, D + 1, D + 2
    assert N == 4 * P and D == 2 * P and HOPS == 3 and B % 2 == 0

    with ExitStack() as ctx:
        def sb(name, shape, dt=F32):
            return ctx.enter_context(nc.sbuf_tensor(name, shape, dt))

        def psum(name, shape):
            return ctx.enter_context(nc.psum_tensor(name, shape, F32))

        def sem(name):
            return ctx.enter_context(nc.semaphore(name))

        hop_ps = psum("hop_ps", [P, 2, 512])
        feat_ps = psum("feat_ps", [P, 2, 512])
        adj_ps = psum("adj_ps", [P, 2, 512])
        xt_ps = psum("xt_ps", [P, 2, 512])

        ident = sb("ident", [P, P])
        minus_half = sb("minus_half", [P, NT])
        minus_one = sb("minus_one", [P, NT])
        var_eps = sb("var_eps", [P, NT])
        w_raw = sb("w_raw", [P, DT, WA + WB])
        w_high = sb("w_high", [P, DT, WA + WB], F32R)
        w_low = sb("w_low", [P, DT, WA + WB], F32R)
        wv_sb = sb("wv_sb", [P, DT, D])
        aw_row = sb("aw_row", [P, 2, D])
        bv_row = sb("bv_row", [P, D])
        bk_row = sb("bk_row", [P, HOPS, D])
        ab_col = sb("ab_col", [P, 1])
        scratch = sb("scratch", [P, D])
        dots = sb("dots", [P, 4])
        bias_row = sb("bias_row", [P, WB])

        x_in = sb("x_in", [P, 2, NT, D])
        x_res = sb("x_res", [P, 2, NT, D])
        a_in = sb("a_in", [P, 2, NT, N])
        xt_high = sb("xt_high", [P, DT, N], F32R)
        xt_low = sb("xt_low", [P, DT, N], F32R)
        xw0 = sb("xw0", [P, 2, NT, WB])
        xw1 = sb("xw1", [P, NT, D])
        g2_high = sb("g2_high", [P, NT, D + 2], F32R)
        g2_low = sb("g2_low", [P, NT, D], F32R)
        si_slope = sb("si_slope", [P, N])
        expo = sb("expo", [P, NT, N])
        alpha = sb("alpha", [P, NT, N])
        alpha_high = sb("alpha_high", [P, 2, NT, N], F32R)
        alpha_low = sb("alpha_low", [P, 2, NT, N], F32R)
        rowsum = sb("rowsum", [P, NT])
        inv_sum = sb("inv_sum", [P, NT])
        g1 = sb("g1", [P, NT, D])
        g1_high = sb("g1_high", [P, NT, D], F32R)
        g1_low = sb("g1_low", [P, NT, D], F32R)
        h = sb("h", [P, 2, D])
        y = sb("y", [P, 2, NT, D])
        stats = sb("stats", [P, NT, 6])
        moments = sb("moments", [P, 2, NT, 2])
        neg_mean = sb("neg_mean", [P, NT])
        variance = sb("variance", [P, NT])
        inv_std = sb("inv_std", [P, 2, NT])
        shift = sb("shift", [P, 2, NT])

        ident_zeroed = sem("ident_zeroed")
        ident_made = sem("ident_made")
        ones_made = sem("ones_made")
        wv_loaded = sem("wv_loaded")
        wk_loaded = sem("wk_loaded")
        rows_loaded = sem("rows_loaded")
        dots_made = sem("dots_made")
        w_folded = sem("w_folded")
        w_high_made = sem("w_high_made")
        w_split = sem("w_split")
        x_loaded = [sem(f"x_loaded{s}") for s in range(2)]
        a_loaded = [sem(f"a_loaded{s}") for s in range(2)]
        stored = [sem(f"stored{s}") for s in range(2)]

        xt_turned = sem("xt_turned")
        featB_done = sem("featB_done")
        featA_done = sem("featA_done")
        si_spread = sem("si_spread")
        adj_turned = sem("adj_turned")
        hop1_done = sem("hop1_done")
        hop2_done = sem("hop2_done")

        xt_high_made = sem("xt_high_made")
        g2_high_made = sem("g2_high_made")
        si_sloped = sem("si_sloped")
        expo_done = sem("expo_done")
        alpha_high_made = sem("alpha_high_made")
        g1_high_made = sem("g1_high_made")
        normalised = sem("normalised")

        xt_split = sem("xt_split")
        feat_out = [sem(f"feat_out{s}") for s in range(2)]
        hop_out = [sem(f"hop_out{s}") for s in range(2)]
        alpha_made = [sem(f"alpha_made{s}") for s in range(2)]
        scores_made = sem("scores_made")
        rowsum_made = sem("rowsum_made")
        inv_sum_made = sem("inv_sum_made")
        y_made = sem("y_made")
        stats_made = sem("stats_made")
        moments_made = sem("moments_made")
        variance_made = sem("variance_made")
        inv_std_made = sem("inv_std_made")
        shift_made = sem("shift_made")

        res_kept = sem("res_kept")
        alpha_split = sem("alpha_split")
        g1_split = sem("g1_split")

        x_d = x.rearrange("b (t p) d -> b p t d", p=P)
        a_d = adj.rearrange("b (t p) j -> b p t j", p=P)
        out_d = out.rearrange("b (t p) d -> b p t d", p=P)
        wk_d = Wk.rearrange("k (t p) e -> k p t e", p=P)
        wv_d = Wv.rearrange("(t p) e -> p t e", p=P)

        block = ctx.enter_context(nc.Block())

        @block.sync
        def _(sp):
            def load_x(n):
                sp.dma_start(x_in[:, n.slot], x_d[n.at]).then_inc(x_loaded[n.slot], 16)

            def load_a(n):
                sp.dma_start(a_in[:, n.slot], a_d[n.at]).then_inc(a_loaded[n.slot], 16)

            def store(b):
                sp.wait_ge(normalised, 4 * (b.at + 1))
                sp.dma_start(out_d[b.at], y[:, b.slot]).then_inc(stored[b.slot], 16)

            load_x(batch(0))
            load_a(batch(0))
            load_x(batch(1))
            load_a(batch(1))
            def iteration(b, m):
                sp.wait_ge(xt_turned, DT * (b.at + 1))
                sp.wait_ge(res_kept, b.at + 1)
                load_x(m)
                sp.wait_ge(adj_turned, NT * (b.at + 1))
                load_a(m)
                store(b)

            iteration(batch(0), batch(2))
            iteration(batch(1), batch(3))
            with sp.Fori(1, B // 2 - 1) as i:
                for ahead in range(2):
                    iteration(in_loop(i, ahead), in_loop(i, ahead + 2))
            store(batch(B - 2))
            store(batch(B - 1))
            for s in range(2):
                sp.wait_ge(stored[s], 16 * (B // 2))

        @block.tensor
        def _(pe):
            def turn_x(m, dt):
                if dt == 0:
                    pe.wait_ge(x_loaded[m.slot], 16 * (m.pair + 1))
                    after(pe, scores_made, NT * m.at)
                else:
                    after(pe, xt_split, DT * m.at)
                for t in range(NT):
                    mm = pe.transpose(xt_ps[:, dt, t * P:(t + 1) * P],
                                      x_in[:, m.slot, t, dt * P:(dt + 1) * P], ident[:, :])
                mm.then_inc(xt_turned, 1)

            def split_product(ps, c0, c1, t):
                for dt in range(DT):
                    xh = xt_high[:, dt, t * P:(t + 1) * P]
                    xl = xt_low[:, dt, t * P:(t + 1) * P]
                    pe.matmul(ps, xh, w_high[:, dt, c0:c1], start=(dt == 0), stop=False)
                    pe.matmul(ps, xh, w_low[:, dt, c0:c1], start=False, stop=False)
                    mm = pe.matmul(ps, xl, w_high[:, dt, c0:c1], start=False, stop=(dt == DT - 1))
                return mm

            def features_b(n, t):
                if t == 0:
                    pe.wait_ge(xt_split, DT * (n.at + 1))
                after(pe, feat_out[t % 2], 4 * n.at + t // 2)
                split_product(feat_ps[:, t % 2, 0:WB], WA, WA + WB, t).then_inc(featB_done, 1)

            def features_a(n, t):
                pe.wait_ge(feat_out[t % 2], 4 * n.at + 2 + t // 2)
                split_product(feat_ps[:, t % 2, 0:WA], 0, WA, t).then_inc(featA_done, 1)

            def spread_si(n):
                pe.wait_ge(feat_out[0], 4 * n.at + 2)
                pe.wait_ge(feat_out[1], 4 * n.at + 2)
                for t in range(NT):
                    mm = pe.transpose(xt_ps[:, 0, t * P:(t + 1) * P],
                                      xw0[:, n.slot, t, SI:SI + 1].to_broadcast([P, P]), ident[:, :])
                mm.then_inc(si_spread, 1)

            def turn_adj(n, j):
                if j == 0:
                    pe.wait_ge(a_loaded[n.slot], 16 * (n.pair + 1))
                after(pe, alpha_made[j % 2], 2 * n.at + j // 2)
                for t in range(NT):
                    mm = pe.transpose(adj_ps[:, j % 2, t * P:(t + 1) * P],
                                      a_in[:, n.slot, t, j * P:(j + 1) * P], ident[:, :])
                mm.then_inc(adj_turned, 1)

            def hop1(b, t):
                if t == 0:
                    pe.wait_ge(alpha_split, NT * (b.at + 1))
                    pe.wait_ge(feat_out[0], 4 * (b.at + 1))
                    pe.wait_ge(feat_out[1], 4 * (b.at + 1))
                after(pe, hop_out[t % 2], 4 * b.at + t // 2)
                ps = hop_ps[:, t % 2, :]
                for j in range(NT):
                    ah = alpha_high[:, b.slot, j, t * P:(t + 1) * P]
                    al = alpha_low[:, b.slot, j, t * P:(t + 1) * P]
                    pe.matmul(ps[:, 0:D + 2], ah, g2_high[:, j, :], start=(j == 0), stop=False)
                    pe.matmul(ps[:, 0:D], ah, g2_low[:, j, :], start=False, stop=False)
                    mm = pe.matmul(ps[:, 0:D + 2], al, g2_high[:, j, :], start=False, stop=(j == NT - 1))
                mm.then_inc(hop1_done, 1)

            def hop2(b, t):
                if t == 0:
                    pe.wait_ge(g1_split, NT * (b.at + 1))
                pe.wait_ge(hop_out[t % 2], 4 * b.at + 2 + t // 2)
                ps = hop_ps[:, t % 2, 0:D]
                for j in range(NT):
                    ah = alpha_high[:, b.slot, j, t * P:(t + 1) * P]
                    al = alpha_low[:, b.slot, j, t * P:(t + 1) * P]
                    pe.matmul(ps, ah, g1_high[:, j, :], start=(j == 0), stop=False)
                    pe.matmul(ps, ah, g1_low[:, j, :], start=False, stop=False)
                    mm = pe.matmul(ps, al, g1_high[:, j, :], start=False, stop=(j == NT - 1))
                mm.then_inc(hop2_done, 1)

            def iteration(b, n=None, m=None):
                for t in range(NT):
                    hop1(b, t)
                    if n:
                        features_b(n, t)
                if n:
                    features_a(n, 0)
                    spread_si(n)
                    features_a(n, 1)
                    features_a(n, 2)
                    turn_adj(n, 0)
                    features_a(n, 3)
                    turn_adj(n, 1)
                hop2(b, 0)
                if n:
                    turn_adj(n, 2)
                hop2(b, 1)
                if n:
                    turn_adj(n, 3)
                if m:
                    turn_x(m, 0)
                hop2(b, 2)
                if m:
                    turn_x(m, 1)
                hop2(b, 3)

            pe.wait_ge(ident_made, 1)
            n = batch(0)
            turn_x(n, 0)
            turn_x(n, 1)
            pe.wait_ge(w_split, 1)
            for t in range(NT):
                features_b(n, t)
            features_a(n, 0)
            spread_si(n)
            for t in range(1, NT):
                features_a(n, t)
            for j in range(NT):
                turn_adj(n, j)
            turn_x(batch(1), 0)
            turn_x(batch(1), 1)
            pe.wait_ge(ones_made, 1)
            iteration(batch(0), batch(1), batch(2))
            iteration(batch(1), batch(2), batch(3))
            with pe.Fori(1, B // 2 - 1) as i:
                for ahead in range(2):
                    iteration(in_loop(i, ahead), in_loop(i, ahead + 1), in_loop(i, ahead + 2))
            iteration(batch(B - 2), batch(B - 1))
            iteration(batch(B - 1))

        @block.scalar
        def _(act):
            def high_x(m, dt):
                act.wait_ge(xt_turned, DT * m.at + dt + 1)
                act.copy(xt_high[:, dt, :], xt_ps[:, dt, :]).then_inc(xt_high_made, 1)

            def high_g2(n, t):
                act.wait_ge(featA_done, NT * n.at + t + 1)
                act.copy(g2_high[:, t, 0:D], feat_ps[:, t % 2, 0:D])
                act.copy(xw1[:, t, :], feat_ps[:, t % 2, D:2 * D]).then_inc(g2_high_made, 1)

            def slope_si(n):
                act.wait_ge(si_spread, n.at + 1)
                act.mul(si_slope[:, :], xt_ps[:, 0, :], SLOPE).then_inc(si_sloped, 1)

            def exponential(n, j):
                act.wait_ge(scores_made, NT * n.at + j + 1)
                act.activation(expo[:, j, :], expo[:, j, :], ACT.Exp,
                               bias=xw0[:, n.slot, j, SJ:SJ + 1]).then_inc(expo_done, 1)

            def high_alpha(n, j):
                act.wait_ge(alpha_made[j % 2], 2 * n.at + j // 2 + 1)
                act.copy(alpha_high[:, n.slot, j, :], alpha[:, j, :]).then_inc(alpha_high_made, 1)

            def high_g1(b, t):
                if t == 0:
                    after(act, hop2_done, NT * b.at)
                act.wait_ge(hop_out[t % 2], 4 * b.at + t // 2 + 1)
                act.copy(g1_high[:, t, :], g1[:, t, :]).then_inc(g1_high_made, 1)

            def normalise(b):
                act.wait_ge(shift_made, b.at + 1)
                for t in range(NT):
                    act.activation(y[:, b.slot, t, :], y[:, b.slot, t, :], ACT.Identity,
                                   bias=shift[:, b.slot, t:t + 1],
                                   scale=inv_std[:, b.slot, t:t + 1]).then_inc(normalised, 1)

            def iteration(b, n=None, m=None):
                for t in range(NT):
                    high_g1(b, t)
                if n:
                    high_g2(n, 0)
                    slope_si(n)
                    high_g2(n, 1)
                    exponential(n, 0)
                    high_g2(n, 2)
                    exponential(n, 1)
                    high_alpha(n, 0)
                    high_g2(n, 3)
                    exponential(n, 2)
                    high_alpha(n, 1)
                    exponential(n, 3)
                    high_alpha(n, 2)
                    high_alpha(n, 3)
                if m:
                    high_x(m, 0)
                    high_x(m, 1)
                normalise(b)

            act.dma_start(wv_sb[:, :, :], wv_d).then_inc(wv_loaded, 16)
            act.dma_start(aw_row[:, :, :].rearrange("p m e -> p (m e)"),
                          aw.rearrange("e o -> (o e)").partition_broadcast(P)).then_inc(rows_loaded, 16)
            act.dma_start(bv_row[:, :], bv.partition_broadcast(P)).then_inc(rows_loaded, 16)
            act.dma_start(ab_col[:, :], ab.partition_broadcast(P)).then_inc(rows_loaded, 16)
            for c, k in enumerate((2, 1, 0)):
                act.dma_start(w_raw[:, :, c * D:(c + 1) * D], wk_d[k]).then_inc(wk_loaded, 16)
            act.dma_start(bk_row[:, :, :].rearrange("p k e -> p (k e)"),
                          bk.rearrange("k e -> (k e)").partition_broadcast(P)).then_inc(rows_loaded, 16)

            n = batch(0)
            high_x(n, 0)
            high_x(n, 1)
            act.wait_ge(w_folded, 1)
            act.copy(w_high[:, :, :], w_raw[:, :, :]).then_inc(w_high_made, 1)
            high_g2(n, 0)
            slope_si(n)
            for t in range(1, NT):
                high_g2(n, t)
            for j in range(NT):
                exponential(n, j)
            for j in range(NT):
                high_alpha(n, j)
            high_x(batch(1), 0)
            high_x(batch(1), 1)
            iteration(batch(0), batch(1), batch(2))
            iteration(batch(1), batch(2), batch(3))
            with act.Fori(1, B // 2 - 1) as i:
                for ahead in range(2):
                    iteration(in_loop(i, ahead), in_loop(i, ahead + 1), in_loop(i, ahead + 2))
            iteration(batch(B - 2), batch(B - 1))
            iteration(batch(B - 1))

        @block.vector
        def _(dve):
            def low_x(m, dt):
                dve.wait_ge(xt_high_made, DT * m.at + dt + 1)
                dve.tensor_tensor(xt_low[:, dt, :], xt_ps[:, dt, :], xt_high[:, dt, :].bitcast(F32),
                                  ALU.subtract).then_inc(xt_split, 1)

            def keep_xw0(n, t):
                dve.wait_ge(featB_done, NT * n.at + t + 1)
                dve.tensor_tensor(xw0[:, n.slot, t, :], feat_ps[:, t % 2, 0:WB], bias_row[:, :],
                                  ALU.add).then_inc(feat_out[t % 2], 1)

            def low_g2(n, t):
                dve.wait_ge(g2_high_made, NT * n.at + t + 1)
                dve.tensor_tensor(g2_low[:, t, :], feat_ps[:, t % 2, 0:D], g2_high[:, t, 0:D].bitcast(F32),
                                  ALU.subtract).then_inc(feat_out[t % 2], 1)

            def score(n, j):
                if j == 0:
                    dve.wait_ge(si_sloped, n.at + 1)
                    after(dve, alpha_made[0], 2 * n.at)
                    after(dve, alpha_made[1], 2 * n.at)
                dve.scalar_tensor_tensor(out=expo[:, j, :], in0=si_slope[:, :],
                                         scalar=xw0[:, n.slot, j, SJ_REST:SJ_REST + 1],
                                         in1=xt_ps[:, 0, :], op0=ALU.add,
                                         op1=ALU.max).then_inc(scores_made, 1)

            def make_alpha(n, j):
                if j == 0:
                    after(dve, alpha_split, NT * n.at)
                dve.wait_ge(adj_turned, NT * n.at + j + 1)
                dve.wait_ge(expo_done, NT * n.at + j + 1)
                dve.tensor_tensor(alpha[:, j, :], adj_ps[:, j % 2, :], expo[:, j, :],
                                  ALU.mult).then_inc(alpha_made[j % 2], 1)

            def leave_hop1(b, t):
                if t == 0:
                    after(dve, g1_split, NT * b.at)
                dve.wait_ge(hop1_done, NT * b.at + t + 1)
                dve.tensor_scalar(rowsum[:, t:t + 1], hop_ps[:, t % 2, D:D + 1], SUM_EPS, None,
                                  ALU.add).then_inc(rowsum_made, 1)
                dve.wait_ge(rowsum_made, NT * b.at + t + 1)
                dve.reciprocal(inv_sum[:, t:t + 1], rowsum[:, t:t + 1]).then_inc(inv_sum_made, 1)
                dve.wait_ge(inv_sum_made, NT * b.at + t + 1)
                dve.scalar_tensor_tensor(out=g1[:, t, :], in0=hop_ps[:, t % 2, 0:D],
                                         scalar=inv_sum[:, t:t + 1], in1=xw1[:, t, :],
                                         op0=ALU.mult, op1=ALU.add).then_inc(hop_out[t % 2], 1)

            def leave_hop2(b, t):
                dve.wait_ge(hop2_done, NT * b.at + t + 1)
                dve.scalar_tensor_tensor(out=h[:, t % 2, :], in0=hop_ps[:, t % 2, 0:D],
                                         scalar=inv_sum[:, t:t + 1], in1=xw0[:, b.slot, t, 0:D],
                                         op0=ALU.mult, op1=ALU.add).then_inc(hop_out[t % 2], 1)

            def add_residual(b, t):
                if t == 0:
                    after(dve, stored[b.slot], 16 * b.pair)
                    dve.wait_ge(res_kept, b.at + 1)
                dve.wait_ge(hop_out[t % 2], 4 * b.at + 2 + t // 2 + 1)
                dve.scalar_tensor_tensor(out=y[:, b.slot, t, :], in0=h[:, t % 2, :], scalar=0.0,
                                         in1=x_res[:, b.slot, t, :], op0=ALU.max,
                                         op1=ALU.add).then_inc(y_made, 1)
                dve.wait_ge(y_made, NT * b.at + t + 1)
                dve.bn_stats(stats[:, t, :], y[:, b.slot, t, :]).then_inc(stats_made, 1)

            def gather_moments(b):
                for t in range(NT):
                    last = dve.bn_aggr(moments[:, b.slot, t, :], stats[:, t, :])
                last.then_inc(moments_made, 1)

            def iteration(b, n=None, m=None):
                for t in range(NT):
                    leave_hop1(b, t)
                    if n:
                        keep_xw0(n, t)
                if n:
                    low_g2(n, 0)
                    score(n, 0)
                    score(n, 1)
                    low_g2(n, 1)
                    score(n, 2)
                    score(n, 3)
                    low_g2(n, 2)
                    make_alpha(n, 0)
                    low_g2(n, 3)
                    make_alpha(n, 1)
                leave_hop2(b, 0)
                add_residual(b, 0)
                if n:
                    make_alpha(n, 2)
                leave_hop2(b, 1)
                add_residual(b, 1)
                if n:
                    make_alpha(n, 3)
                if m:
                    low_x(m, 0)
                leave_hop2(b, 2)
                add_residual(b, 2)
                leave_hop2(b, 3)
                add_residual(b, 3)
                dve.wait_ge(stats_made, NT * (b.at + 1))
                if m:
                    low_x(m, 1)
                gather_moments(b)

            n = batch(0)
            dve.memset(bias_row[:, SI:WB], 0.0)
            dve.memset(w_raw[:, :, WA + SI + 1:WA + WB], 0.0)
            dve.wait_ge(wv_loaded, 16)
            dve.wait_ge(rows_loaded, 4 * 16)
            made = 0
            for half, column in enumerate((WA + SJ, WA + SI)):
                for dt in range(DT):
                    made += 1
                    dve.tensor_tensor_reduce(scratch[:, :], wv_sb[:, dt, :], aw_row[:, half, :], 1.0, 0.0,
                                             ALU.mult, ALU.add,
                                             w_raw[:, dt, column:column + 1]).then_inc(dots_made, 1)
                    dve.wait_ge(dots_made, made)
                made += 1
                dve.tensor_tensor_reduce(scratch[:, :], bv_row[:, :], aw_row[:, half, :], 1.0, 0.0,
                                         ALU.mult, ALU.add, dots[:, half:half + 1]).then_inc(dots_made, 1)
                dve.wait_ge(dots_made, made)
            dve.tensor_scalar(w_raw[:, :, WA + SJ_REST], w_raw[:, :, WA + SJ], SLOPE - 1.0, None, ALU.mult)
            dve.tensor_tensor(scratch[:, :], bk_row[:, 0, :], bk_row[:, 1, :], ALU.add).then_inc(dots_made, 1)
            dve.tensor_tensor(dots[:, 2:3], dots[:, 0:1], dots[:, 1:2], ALU.add).then_inc(dots_made, 1)
            dve.wait_ge(dots_made, made + 2)
            dve.tensor_tensor(bias_row[:, SJ:SJ + 1], dots[:, 2:3], ab_col[:, :], ALU.add).then_inc(dots_made, 1)
            dve.wait_ge(dots_made, made + 3)
            dve.tensor_scalar(bias_row[:, SJ_REST:SJ_REST + 1], bias_row[:, SJ:SJ + 1], SLOPE - 1.0, None,
                              ALU.mult)
            dve.wait_ge(wk_loaded, 3 * 16)
            dve.tensor_tensor(bias_row[:, 0:D], scratch[:, :], bk_row[:, 2, :], ALU.add).then_inc(w_folded, 1)
            dve.wait_ge(w_folded, 1)
            low_x(n, 0)
            low_x(n, 1)
            dve.wait_ge(w_high_made, 1)
            dve.tensor_tensor(w_low[:, :, :], w_raw[:, :, :], w_high[:, :, :].bitcast(F32),
                              ALU.subtract).then_inc(w_split, 1)
            for t in range(NT):
                keep_xw0(n, t)
            low_g2(n, 0)
            for j in range(NT):
                score(n, j)
            for t in range(1, NT):
                low_g2(n, t)
            for j in range(NT):
                make_alpha(n, j)
            low_x(batch(1), 0)
            low_x(batch(1), 1)
            iteration(batch(0), batch(1), batch(2))
            iteration(batch(1), batch(2), batch(3))
            with dve.Fori(1, B // 2 - 1) as i:
                for ahead in range(2):
                    iteration(in_loop(i, ahead), in_loop(i, ahead + 1), in_loop(i, ahead + 2))
            iteration(batch(B - 2), batch(B - 1))
            iteration(batch(B - 1))

        @block.gpsimd
        def _(pool):
            def low_g1(b, t):
                pool.wait_ge(g1_high_made, NT * b.at + t + 1)
                pool.tensor_tensor(g1_low[:, t, :], g1[:, t, :], g1_high[:, t, :].bitcast(F32),
                                   ALU.subtract).then_inc(g1_split, 1)

            def keep_residual(n):
                pool.tensor_copy(x_res[:, n.slot], x_in[:, n.slot]).then_inc(res_kept, 1)

            def low_alpha(n, j):
                pool.wait_ge(alpha_high_made, NT * n.at + j + 1)
                pool.tensor_tensor(alpha_low[:, n.slot, j, :], alpha[:, j, :],
                                   alpha_high[:, n.slot, j, :].bitcast(F32),
                                   ALU.subtract).then_inc(alpha_split, 1)

            def norm_factors(b):
                pool.wait_ge(moments_made, b.at + 1)
                pool.tensor_tensor(neg_mean[:, :], moments[:, b.slot, :, 0], minus_one[:, :], ALU.mult)
                pool.tensor_tensor(variance[:, :], moments[:, b.slot, :, 1], var_eps[:, :],
                                   ALU.add).then_inc(variance_made, 1)
                pool.wait_ge(variance_made, b.at + 1)
                pool.tensor_tensor(inv_std[:, b.slot, :], variance[:, :], minus_half[:, :],
                                   ALU.pow).then_inc(inv_std_made, 1)
                pool.wait_ge(inv_std_made, b.at + 1)
                pool.tensor_tensor(shift[:, b.slot, :], neg_mean[:, :], inv_std[:, b.slot, :],
                                   ALU.mult).then_inc(shift_made, 1)

            def iteration(b, n=None):
                if n:
                    pool.wait_ge(x_loaded[n.slot], 16 * (n.pair + 1))
                    after(pool, y_made, NT * b.at)
                for t in range(NT):
                    low_g1(b, t)
                if n:
                    keep_residual(n)
                    for j in range(NT):
                        low_alpha(n, j)
                norm_factors(b)

            pool.memset(minus_half[:, :], -0.5)
            pool.memset(minus_one[:, :], -1.0)
            pool.memset(var_eps[:, :], VAR_EPS)
            pool.memset(ident[:, :], 0.0).then_inc(ident_zeroed, 1)
            pool.wait_ge(ident_zeroed, 1)
            pool.affine_select(out=ident[:, :], in_=ident[:, :], compare_op=ALU.not_equal, fill=1.0,
                               base=0, pattern=[[-1, P]], channel_multiplier=1).then_inc(ident_made, 1)
            pool.memset(g2_high[:, :, D:D + 2].bitcast(F32), 1.0).then_inc(ones_made, 1)
            n = batch(0)
            pool.wait_ge(x_loaded[0], 16)
            keep_residual(n)
            for j in range(NT):
                low_alpha(n, j)
            iteration(batch(0), batch(1))
            iteration(batch(1), batch(2))
            with pool.Fori(1, B // 2 - 1) as i:
                for ahead in range(2):
                    iteration(in_loop(i, ahead), in_loop(i, ahead + 1))
            iteration(batch(B - 2), batch(B - 1))
            iteration(batch(B - 1))


_INS = ["x", "adj", "L0_gnn_Wv", "L0_gnn_bv", "L0_gnn_aw", "L0_gnn_ab", "L0_gnn_Wk", "L0_gnn_bk"]


def kernel(**inputs):
    import numpy as _np
    import concourse.bacc as _bacc
    from concourse import mybir as _mybir
    from concourse.bass_utils import run_bass_kernel_spmd as _run

    nc = _bacc.Bacc("TRN2", target_bir_lowering=False, num_devices=1)
    arrays, args = {}, []
    for name in _INS:
        a = _np.ascontiguousarray(inputs[name])
        arrays[f"in_{name}_dram"] = a
        args.append(nc.dram_tensor(f"in_{name}_dram", a.shape, _mybir.dt.from_np(a.dtype), kind="ExternalInput").ap())
    shape = arrays["in_x_dram"].shape
    args.append(nc.dram_tensor("out_0_dram", shape, _mybir.dt.float32, kind="ExternalOutput").ap())
    gnn_resnorm(nc, *args)
    r = _run(nc, [arrays], core_ids=[0])
    return r.results[0]["out_0_dram"]
```

```python
from collections import namedtuple
from contextlib import ExitStack

from concourse import mybir

ALU = mybir.AluOpType
ACT = mybir.ActivationFunctionType
F32 = mybir.dt.float32
F32R = mybir.dt.float32r

P = 128
SLOPE = 0.2
SUM_EPS = 1e-12
VAR_EPS = 1e-5

Batch = namedtuple("Batch", "at pair slot")


def batch(number):
    return Batch(number, number // 2, number % 2)


FIRST = batch(0)


def in_loop(i, ahead):
    return Batch(2 * i + ahead, i + ahead // 2, ahead % 2)


def after(engine, semaphore, count):
    if not isinstance(count, int) or count > 0:
        engine.wait_ge(semaphore, count)


def gnn_resnorm(nc, x, adj, Wv, bv, aw, ab, Wk, bk, out):
    B, N, D = x.shape
    HOPS = Wk.shape[0]
    NT = N // P
    DT = D // P
    WA = 2 * D
    WB = D + 4
    SJ, SJ_REST, SI = D, D + 1, D + 2
    assert N == 4 * P and D == 2 * P and HOPS == 3 and B % 2 == 0

    with ExitStack() as ctx:
        def sb(name, shape, dt=F32):
            return ctx.enter_context(nc.sbuf_tensor(name, shape, dt))

        def psum(name, shape):
            return ctx.enter_context(nc.psum_tensor(name, shape, F32))

        def sem(name):
            return ctx.enter_context(nc.semaphore(name))

        hop_ps = psum("hop_ps", [P, 2, 512])
        feat_ps = psum("feat_ps", [P, 2, 512])
        adj_ps = psum("adj_ps", [P, 2, 512])
        xt_ps = psum("xt_ps", [P, 2, 512])

        ident = sb("ident", [P, P])
        minus_half = sb("minus_half", [P, NT])
        minus_one = sb("minus_one", [P, NT])
        var_eps = sb("var_eps", [P, NT])
        w_raw = sb("w_raw", [P, DT, WA + WB])
        w_high = sb("w_high", [P, DT, WA + WB], F32R)
        w_low = sb("w_low", [P, DT, WA + WB], F32R)
        wv_sb = sb("wv_sb", [P, DT, D])
        aw_row = sb("aw_row", [P, 2, D])
        bv_row = sb("bv_row", [P, D])
        bk_row = sb("bk_row", [P, HOPS, D])
        ab_col = sb("ab_col", [P, 1])
        scratch = sb("scratch", [P, D])
        dots = sb("dots", [P, 4])
        bias_row = sb("bias_row", [P, WB])

        x_in = sb("x_in", [P, 2, NT, D])
        x_res = sb("x_res", [P, 2, NT, D])
        a_in = sb("a_in", [P, 2, NT, N])
        xt_high = sb("xt_high", [P, DT, N], F32R)
        xt_low = sb("xt_low", [P, DT, N], F32R)
        xw0 = sb("xw0", [P, 2, NT, WB])
        xw1 = sb("xw1", [P, NT, D])
        g2_high = sb("g2_high", [P, NT, D + 2], F32R)
        g2_low = sb("g2_low", [P, NT, D], F32R)
        si_slope = sb("si_slope", [P, N])
        expo = sb("expo", [P, NT, N])
        alpha = sb("alpha", [P, NT, N])
        alpha_high = sb("alpha_high", [P, 2, NT, N], F32R)
        alpha_low = sb("alpha_low", [P, 2, NT, N], F32R)
        rowsum = sb("rowsum", [P, NT])
        inv_sum = sb("inv_sum", [P, NT])
        g1 = sb("g1", [P, NT, D])
        g1_high = sb("g1_high", [P, NT, D], F32R)
        g1_low = sb("g1_low", [P, NT, D], F32R)
        h = sb("h", [P, 2, D])
        y = sb("y", [P, 2, NT, D])
        stats = sb("stats", [P, NT, 6])
        moments = sb("moments", [P, 2, NT, 2])
        neg_mean = sb("neg_mean", [P, NT])
        variance = sb("variance", [P, NT])
        inv_std = sb("inv_std", [P, 2, NT])
        shift = sb("shift", [P, 2, NT])

        ident_zeroed = sem("ident_zeroed")
        ident_made = sem("ident_made")
        ones_made = sem("ones_made")
        wv_loaded = sem("wv_loaded")
        wk_loaded = sem("wk_loaded")
        w0_loaded = sem("w0_loaded")
        rows_loaded = sem("rows_loaded")
        dots_made = sem("dots_made")
        w_folded = sem("w_folded")
        w_high_made = sem("w_high_made")
        w_split = sem("w_split")
        x_loaded = [sem(f"x_loaded{s}") for s in range(2)]
        a_loaded = [sem(f"a_loaded{s}") for s in range(2)]
        stored = [sem(f"stored{s}") for s in range(2)]

        xt_turned = sem("xt_turned")
        featB_done = sem("featB_done")
        featA_done = sem("featA_done")
        si_spread = sem("si_spread")
        adj_turned = sem("adj_turned")
        hop1_done = sem("hop1_done")
        hop2_done = sem("hop2_done")

        xt_high_made = sem("xt_high_made")
        g2_high_made = sem("g2_high_made")
        si_sloped = sem("si_sloped")
        expo_done = sem("expo_done")
        alpha_high_made = sem("alpha_high_made")
        g1_high_made = sem("g1_high_made")
        normalised = sem("normalised")

        xt_split = sem("xt_split")
        feat_out = [sem(f"feat_out{s}") for s in range(2)]
        hop_out = [sem(f"hop_out{s}") for s in range(2)]
        alpha_made = [sem(f"alpha_made{s}") for s in range(2)]
        scores_made = sem("scores_made")
        rowsum_made = sem("rowsum_made")
        inv_sum_made = sem("inv_sum_made")
        y_made = sem("y_made")
        stats_made = sem("stats_made")
        moments_made = sem("moments_made")
        variance_made = sem("variance_made")
        inv_std_made = sem("inv_std_made")
        shift_made = sem("shift_made")

        res_kept = sem("res_kept")
        alpha_split = sem("alpha_split")
        g1_split = sem("g1_split")

        x_d = x.rearrange("b (t p) d -> b p t d", p=P)
        a_d = adj.rearrange("b (t p) j -> b p t j", p=P)
        out_d = out.rearrange("b (t p) d -> b p t d", p=P)
        wk_d = Wk.rearrange("k (t p) e -> k p t e", p=P)
        wv_d = Wv.rearrange("(t p) e -> p t e", p=P)

        block = ctx.enter_context(nc.Block())

        @block.sync
        def _(sp):
            def load_x(n):
                sp.dma_start(x_in[:, n.slot], x_d[n.at]).then_inc(x_loaded[n.slot], 16)

            def load_a(n):
                sp.dma_start(a_in[:, n.slot], a_d[n.at]).then_inc(a_loaded[n.slot], 16)

            def replace(n):
                m = Batch(n.at + 2, n.pair + 1, n.slot)
                sp.wait_ge(adj_turned, NT * (n.at + 1))
                load_a(m)
                sp.wait_ge(xt_turned, DT * (n.at + 1))
                sp.wait_ge(res_kept, n.at + 1)
                load_x(m)

            def store(b):
                sp.wait_ge(normalised, NT * (b.at + 1))
                sp.dma_start(out_d[b.at], y[:, b.slot]).then_inc(stored[b.slot], 16)

            load_x(batch(0))
            for c, k in enumerate((2, 1)):
                sp.dma_start(w_raw[:, :, c * D:(c + 1) * D], wk_d[k]).then_inc(wk_loaded, 16)
            sp.dma_start(wv_sb[:, :, :], wv_d).then_inc(wv_loaded, 16)
            sp.dma_start(w_raw[:, :, WA:WA + D], wk_d[0]).then_inc(w0_loaded, 16)
            load_a(batch(0))
            load_x(batch(1))
            load_a(batch(1))
            replace(batch(0))
            replace(batch(1))
            with sp.Fori(1, B // 2 - 1) as i:
                for ahead in range(2):
                    replace(in_loop(i, ahead))
                    store(in_loop(i, ahead - 2))
            for b in range(B - 4, B):
                store(batch(b))
            for s in range(2):
                sp.wait_ge(stored[s], 16 * (B // 2))

        @block.tensor
        def _(pe):
            def turn_x(m, dt):
                if dt == 0:
                    pe.wait_ge(x_loaded[m.slot], 16 * (m.pair + 1))
                    after(pe, scores_made, NT * m.at)
                else:
                    after(pe, xt_split, DT * m.at)
                for t in range(NT):
                    mm = pe.transpose(xt_ps[:, dt, t * P:(t + 1) * P],
                                      x_in[:, m.slot, t, dt * P:(dt + 1) * P], ident[:, :])
                mm.then_inc(xt_turned, 1)

            def split_product(ps, c0, c1, t):
                for dt in range(DT):
                    xh = xt_high[:, dt, t * P:(t + 1) * P]
                    xl = xt_low[:, dt, t * P:(t + 1) * P]
                    pe.matmul(ps, xh, w_high[:, dt, c0:c1], start=(dt == 0), stop=False)
                    pe.matmul(ps, xh, w_low[:, dt, c0:c1], start=False, stop=False)
                    mm = pe.matmul(ps, xl, w_high[:, dt, c0:c1], start=False, stop=(dt == DT - 1))
                return mm

            def features_b(n, t):
                if t == 0 and n is not FIRST:
                    pe.wait_ge(xt_split, DT * (n.at + 1))
                pe.wait_ge(feat_out[t % 2], 4 * n.at + (2 if n is FIRST else 0) + t // 2)
                split_product(feat_ps[:, t % 2, 0:WB], WA, WA + WB, t).then_inc(featB_done, 1)

            def features_a(n, t):
                after(pe, feat_out[t % 2], 4 * n.at + (0 if n is FIRST else 2) + t // 2)
                split_product(feat_ps[:, t % 2, 0:WA], 0, WA, t).then_inc(featA_done, 1)

            def spread_si(n):
                done = 4 if n is FIRST else 4 * n.at + 2
                pe.wait_ge(feat_out[0], done)
                pe.wait_ge(feat_out[1], done)
                for t in range(NT):
                    mm = pe.transpose(xt_ps[:, 0, t * P:(t + 1) * P],
                                      xw0[:, n.slot, t, SI:SI + 1].to_broadcast([P, P]), ident[:, :])
                mm.then_inc(si_spread, 1)

            def turn_adj(n, j):
                if j == 0:
                    pe.wait_ge(a_loaded[n.slot], 16 * (n.pair + 1))
                after(pe, alpha_made[j % 2], 2 * n.at + j // 2)
                for t in range(NT):
                    mm = pe.transpose(adj_ps[:, j % 2, t * P:(t + 1) * P],
                                      a_in[:, n.slot, t, j * P:(j + 1) * P], ident[:, :])
                mm.then_inc(adj_turned, 1)

            def hop1(b, t):
                if t == 0:
                    pe.wait_ge(alpha_split, NT * (b.at + 1))
                    pe.wait_ge(feat_out[0], 4 * (b.at + 1))
                    pe.wait_ge(feat_out[1], 4 * (b.at + 1))
                after(pe, hop_out[t % 2], 4 * b.at + t // 2)
                ps = hop_ps[:, t % 2, :]
                for j in range(NT):
                    ah = alpha_high[:, b.slot, j, t * P:(t + 1) * P]
                    al = alpha_low[:, b.slot, j, t * P:(t + 1) * P]
                    pe.matmul(ps[:, 0:D + 2], ah, g2_high[:, j, :], start=(j == 0), stop=False)
                    pe.matmul(ps[:, 0:D], ah, g2_low[:, j, :], start=False, stop=False)
                    mm = pe.matmul(ps[:, 0:D + 2], al, g2_high[:, j, :], start=False, stop=(j == NT - 1))
                mm.then_inc(hop1_done, 1)

            def hop2(b, t):
                if t == 0:
                    pe.wait_ge(g1_split, NT * (b.at + 1))
                pe.wait_ge(hop_out[t % 2], 4 * b.at + 2 + t // 2)
                ps = hop_ps[:, t % 2, 0:D]
                for j in range(NT):
                    ah = alpha_high[:, b.slot, j, t * P:(t + 1) * P]
                    al = alpha_low[:, b.slot, j, t * P:(t + 1) * P]
                    pe.matmul(ps, ah, g1_high[:, j, :], start=(j == 0), stop=False)
                    pe.matmul(ps, ah, g1_low[:, j, :], start=False, stop=False)
                    mm = pe.matmul(ps, al, g1_high[:, j, :], start=False, stop=(j == NT - 1))
                mm.then_inc(hop2_done, 1)

            def iteration(b, n=None, m=None):
                hop1(b, 0)
                hop1(b, 1)
                if n:
                    spread_si(n)
                hop1(b, 2)
                hop1(b, 3)
                if n:
                    for t in range(NT - 1):
                        features_a(n, t)
                        turn_adj(n, t)
                    features_a(n, NT - 1)
                if m:
                    turn_x(m, 0)
                    turn_x(m, 1)
                if n:
                    turn_adj(n, NT - 1)
                for t in range(NT):
                    hop2(b, t)
                    if m:
                        features_b(m, t)

            pe.wait_ge(ident_made, 1)
            n = FIRST
            turn_x(n, 0)
            turn_x(n, 1)
            pe.wait_ge(xt_split, DT)
            pe.wait_ge(w_split, 1)
            for t in range(NT):
                features_a(n, t)
            pe.wait_ge(w_split, 2)
            for t in range(NT):
                features_b(n, t)
            turn_adj(n, 0)
            turn_adj(n, 1)
            spread_si(n)
            turn_adj(n, 2)
            turn_adj(n, 3)
            n = batch(1)
            turn_x(n, 0)
            turn_x(n, 1)
            for t in range(NT):
                features_b(n, t)
            pe.wait_ge(ones_made, 1)
            iteration(batch(0), batch(1), batch(2))
            iteration(batch(1), batch(2), batch(3))
            with pe.Fori(1, B // 2 - 1) as i:
                for ahead in range(2):
                    iteration(in_loop(i, ahead), in_loop(i, ahead + 1), in_loop(i, ahead + 2))
            iteration(batch(B - 2), batch(B - 1))
            iteration(batch(B - 1))

        @block.scalar
        def _(act):
            def high_x(m, dt):
                act.wait_ge(xt_turned, DT * m.at + dt + 1)
                act.copy(xt_high[:, dt, :], xt_ps[:, dt, :]).then_inc(xt_high_made, 1)

            def high_g2(n, t):
                act.wait_ge(featA_done, NT * n.at + t + 1)
                act.copy(g2_high[:, t, 0:D], feat_ps[:, t % 2, 0:D])
                act.copy(xw1[:, t, :], feat_ps[:, t % 2, D:2 * D]).then_inc(g2_high_made, 1)

            def slope_si(n):
                act.wait_ge(si_spread, n.at + 1)
                act.mul(si_slope[:, :], xt_ps[:, 0, :], SLOPE).then_inc(si_sloped, 1)

            def exponential(n, j):
                act.wait_ge(scores_made, NT * n.at + j + 1)
                act.activation(expo[:, j, :], expo[:, j, :], ACT.Exp,
                               bias=xw0[:, n.slot, j, SJ:SJ + 1]).then_inc(expo_done, 1)

            def high_alpha(n, j):
                act.wait_ge(alpha_made[j % 2], 2 * n.at + j // 2 + 1)
                act.copy(alpha_high[:, n.slot, j, :], alpha[:, j, :]).then_inc(alpha_high_made, 1)

            def high_g1(b, t):
                if t == 0:
                    after(act, hop2_done, NT * b.at)
                act.wait_ge(hop_out[t % 2], 4 * b.at + t // 2 + 1)
                act.copy(g1_high[:, t, :], g1[:, t, :]).then_inc(g1_high_made, 1)

            def normalise(b):
                act.wait_ge(shift_made, b.at + 1)
                for t in range(NT):
                    act.activation(y[:, b.slot, t, :], y[:, b.slot, t, :], ACT.Identity,
                                   bias=shift[:, b.slot, t:t + 1],
                                   scale=inv_std[:, b.slot, t:t + 1]).then_inc(normalised, 1)

            def keep_residual(n):
                act.wait_ge(x_loaded[n.slot], 16 * (n.pair + 1))
                after(act, y_made, NT * (n.at - 1))
                act.copy(x_res[:, n.slot], x_in[:, n.slot]).then_inc(res_kept, 1)

            def iteration(b, n=None, m=None, last=None):
                high_g1(b, 0)
                high_g1(b, 1)
                if n:
                    slope_si(n)
                high_g1(b, 2)
                if n:
                    exponential(n, 0)
                high_g1(b, 3)
                if n:
                    exponential(n, 1)
                    high_g2(n, 0)
                    exponential(n, 2)
                    exponential(n, 3)
                    for t in range(1, NT):
                        high_g2(n, t)
                        if t < NT - 1:
                            high_alpha(n, t - 1)
                if m:
                    high_x(m, 0)
                    high_x(m, 1)
                if n:
                    high_alpha(n, NT - 2)
                    high_alpha(n, NT - 1)
                    keep_residual(n)
                if last:
                    normalise(last)

            act.dma_start(aw_row[:, :, :].rearrange("p m e -> p (m e)"),
                          aw.rearrange("e o -> (o e)").partition_broadcast(P)).then_inc(rows_loaded, 16)
            act.dma_start(bv_row[:, :], bv.partition_broadcast(P)).then_inc(rows_loaded, 16)
            act.dma_start(ab_col[:, :], ab.partition_broadcast(P)).then_inc(rows_loaded, 16)
            act.dma_start(bk_row[:, :, :].rearrange("p k e -> p (k e)"),
                          bk.rearrange("k e -> (k e)").partition_broadcast(P)).then_inc(rows_loaded, 16)

            n = FIRST
            high_x(n, 0)
            high_x(n, 1)
            act.wait_ge(wk_loaded, 2 * 16)
            act.copy(w_high[:, :, 0:WA], w_raw[:, :, 0:WA]).then_inc(w_high_made, 1)
            for t in range(NT):
                high_g2(n, t)
            act.wait_ge(w_folded, 1)
            act.copy(w_high[:, :, WA:], w_raw[:, :, WA:]).then_inc(w_high_made, 1)
            keep_residual(n)
            slope_si(n)
            for j in range(NT):
                exponential(n, j)
            for j in range(NT):
                high_alpha(n, j)
            high_x(batch(1), 0)
            high_x(batch(1), 1)
            iteration(batch(0), batch(1), batch(2))
            iteration(batch(1), batch(2), batch(3), batch(0))
            with act.Fori(1, B // 2 - 1) as i:
                for ahead in range(2):
                    iteration(in_loop(i, ahead), in_loop(i, ahead + 1), in_loop(i, ahead + 2),
                              in_loop(i, ahead - 1))
            iteration(batch(B - 2), batch(B - 1), None, batch(B - 3))
            iteration(batch(B - 1), None, None, batch(B - 2))
            normalise(batch(B - 1))

        @block.vector
        def _(dve):
            def low_x(m, dt):
                dve.wait_ge(xt_high_made, DT * m.at + dt + 1)
                dve.tensor_tensor(xt_low[:, dt, :], xt_ps[:, dt, :], xt_high[:, dt, :].bitcast(F32),
                                  ALU.subtract).then_inc(xt_split, 1)

            def keep_xw0(n, t):
                dve.wait_ge(featB_done, NT * n.at + t + 1)
                dve.tensor_tensor(xw0[:, n.slot, t, :], feat_ps[:, t % 2, 0:WB], bias_row[:, :],
                                  ALU.add).then_inc(feat_out[t % 2], 1)

            def low_g2(n, t):
                dve.wait_ge(g2_high_made, NT * n.at + t + 1)
                dve.tensor_tensor(g2_low[:, t, :], feat_ps[:, t % 2, 0:D], g2_high[:, t, 0:D].bitcast(F32),
                                  ALU.subtract).then_inc(feat_out[t % 2], 1)

            def score(n, j):
                if j == 0:
                    dve.wait_ge(si_sloped, n.at + 1)
                    after(dve, alpha_made[0], 2 * n.at)
                    after(dve, alpha_made[1], 2 * n.at)
                dve.scalar_tensor_tensor(out=expo[:, j, :], in0=si_slope[:, :],
                                         scalar=xw0[:, n.slot, j, SJ_REST:SJ_REST + 1],
                                         in1=xt_ps[:, 0, :], op0=ALU.add,
                                         op1=ALU.max).then_inc(scores_made, 1)

            def make_alpha(n, j):
                if j == 0:
                    after(dve, alpha_split, NT * n.at)
                dve.wait_ge(adj_turned, NT * n.at + j + 1)
                dve.wait_ge(expo_done, NT * n.at + j + 1)
                dve.tensor_tensor(alpha[:, j, :], adj_ps[:, j % 2, :], expo[:, j, :],
                                  ALU.mult).then_inc(alpha_made[j % 2], 1)

            def leave_hop1(b, t):
                if t == 0:
                    after(dve, g1_split, NT * b.at)
                dve.wait_ge(hop1_done, NT * b.at + t + 1)
                dve.tensor_scalar(rowsum[:, t:t + 1], hop_ps[:, t % 2, D:D + 1], SUM_EPS, None,
                                  ALU.add).then_inc(rowsum_made, 1)
                dve.wait_ge(rowsum_made, NT * b.at + t + 1)
                dve.reciprocal(inv_sum[:, t:t + 1], rowsum[:, t:t + 1]).then_inc(inv_sum_made, 1)
                dve.wait_ge(inv_sum_made, NT * b.at + t + 1)
                dve.scalar_tensor_tensor(out=g1[:, t, :], in0=hop_ps[:, t % 2, 0:D],
                                         scalar=inv_sum[:, t:t + 1], in1=xw1[:, t, :],
                                         op0=ALU.mult, op1=ALU.add).then_inc(hop_out[t % 2], 1)

            def leave_hop2(b, t):
                dve.wait_ge(hop2_done, NT * b.at + t + 1)
                dve.scalar_tensor_tensor(out=h[:, t % 2, :], in0=hop_ps[:, t % 2, 0:D],
                                         scalar=inv_sum[:, t:t + 1], in1=xw0[:, b.slot, t, 0:D],
                                         op0=ALU.mult, op1=ALU.add).then_inc(hop_out[t % 2], 1)

            def add_residual(b, t):
                if t == 0:
                    after(dve, stored[b.slot], 16 * b.pair)
                    dve.wait_ge(res_kept, b.at + 1)
                dve.wait_ge(hop_out[t % 2], 4 * b.at + 2 + t // 2 + 1)
                dve.scalar_tensor_tensor(out=y[:, b.slot, t, :], in0=h[:, t % 2, :], scalar=0.0,
                                         in1=x_res[:, b.slot, t, :], op0=ALU.max,
                                         op1=ALU.add).then_inc(y_made, 1)
                dve.wait_ge(y_made, NT * b.at + t + 1)
                dve.bn_stats(stats[:, t, :], y[:, b.slot, t, :]).then_inc(stats_made, 1)

            def gather_moments(b):
                for t in range(NT):
                    last = dve.bn_aggr(moments[:, b.slot, t, :], stats[:, t, :])
                last.then_inc(moments_made, 1)

            def iteration(b, n=None, m=None):
                leave_hop1(b, 0)
                leave_hop1(b, 1)
                if n:
                    score(n, 0)
                leave_hop1(b, 2)
                if n:
                    score(n, 1)
                leave_hop1(b, 3)
                if n:
                    score(n, 2)
                    score(n, 3)
                    for t in range(NT - 1):
                        low_g2(n, t)
                        make_alpha(n, t)
                    low_g2(n, NT - 1)
                if m:
                    low_x(m, 0)
                    low_x(m, 1)
                if n:
                    make_alpha(n, NT - 1)
                for t in range(NT):
                    leave_hop2(b, t)
                    add_residual(b, t)
                    if t == NT - 1:
                        dve.wait_ge(stats_made, NT * (b.at + 1))
                    if m:
                        keep_xw0(m, t)
                gather_moments(b)

            n = FIRST
            dve.memset(bias_row[:, SI:WB], 0.0)
            dve.memset(w_raw[:, :, WA + SI + 1:WA + WB], 0.0)
            low_x(n, 0)
            low_x(n, 1)
            dve.wait_ge(w_high_made, 1)
            dve.tensor_tensor(w_low[:, :, 0:WA], w_raw[:, :, 0:WA], w_high[:, :, 0:WA].bitcast(F32),
                              ALU.subtract).then_inc(w_split, 1)
            dve.wait_ge(wv_loaded, 16)
            dve.wait_ge(rows_loaded, 4 * 16)
            made = 0
            for half, column in enumerate((WA + SJ, WA + SI)):
                for dt in range(DT):
                    made += 1
                    dve.tensor_tensor_reduce(scratch[:, :], wv_sb[:, dt, :], aw_row[:, half, :], 1.0, 0.0,
                                             ALU.mult, ALU.add,
                                             w_raw[:, dt, column:column + 1]).then_inc(dots_made, 1)
                    dve.wait_ge(dots_made, made)
                made += 1
                dve.tensor_tensor_reduce(scratch[:, :], bv_row[:, :], aw_row[:, half, :], 1.0, 0.0,
                                         ALU.mult, ALU.add, dots[:, half:half + 1]).then_inc(dots_made, 1)
                dve.wait_ge(dots_made, made)
            dve.tensor_scalar(w_raw[:, :, WA + SJ_REST], w_raw[:, :, WA + SJ], SLOPE - 1.0, None, ALU.mult)
            dve.tensor_tensor(scratch[:, :], bk_row[:, 0, :], bk_row[:, 1, :], ALU.add).then_inc(dots_made, 1)
            dve.tensor_tensor(dots[:, 2:3], dots[:, 0:1], dots[:, 1:2], ALU.add).then_inc(dots_made, 1)
            dve.wait_ge(dots_made, made + 2)
            dve.tensor_tensor(bias_row[:, SJ:SJ + 1], dots[:, 2:3], ab_col[:, :], ALU.add).then_inc(dots_made, 1)
            dve.wait_ge(dots_made, made + 3)
            dve.tensor_scalar(bias_row[:, SJ_REST:SJ_REST + 1], bias_row[:, SJ:SJ + 1], SLOPE - 1.0, None,
                              ALU.mult)
            dve.wait_ge(w0_loaded, 16)
            dve.tensor_tensor(bias_row[:, 0:D], scratch[:, :], bk_row[:, 2, :], ALU.add).then_inc(w_folded, 1)
            low_g2(n, 0)
            low_g2(n, 1)
            dve.wait_ge(w_high_made, 2)
            dve.tensor_tensor(w_low[:, :, WA:], w_raw[:, :, WA:], w_high[:, :, WA:].bitcast(F32),
                              ALU.subtract).then_inc(w_split, 1)
            low_g2(n, 2)
            low_g2(n, 3)
            for t in range(NT):
                keep_xw0(n, t)
            for j in range(NT):
                score(n, j)
            for j in range(NT):
                make_alpha(n, j)
            n = batch(1)
            low_x(n, 0)
            low_x(n, 1)
            for t in range(NT):
                keep_xw0(n, t)
            iteration(batch(0), batch(1), batch(2))
            iteration(batch(1), batch(2), batch(3))
            with dve.Fori(1, B // 2 - 1) as i:
                for ahead in range(2):
                    iteration(in_loop(i, ahead), in_loop(i, ahead + 1), in_loop(i, ahead + 2))
            iteration(batch(B - 2), batch(B - 1))
            iteration(batch(B - 1))

        @block.gpsimd
        def _(pool):
            def low_g1(b, t):
                pool.wait_ge(g1_high_made, NT * b.at + t + 1)
                pool.tensor_tensor(g1_low[:, t, :], g1[:, t, :], g1_high[:, t, :].bitcast(F32),
                                   ALU.subtract).then_inc(g1_split, 1)

            def low_alpha(n, j):
                pool.wait_ge(alpha_high_made, NT * n.at + j + 1)
                pool.tensor_tensor(alpha_low[:, n.slot, j, :], alpha[:, j, :],
                                   alpha_high[:, n.slot, j, :].bitcast(F32),
                                   ALU.subtract).then_inc(alpha_split, 1)

            def norm_factors(b):
                pool.wait_ge(moments_made, b.at + 1)
                pool.tensor_tensor(neg_mean[:, :], moments[:, b.slot, :, 0], minus_one[:, :], ALU.mult)
                pool.tensor_tensor(variance[:, :], moments[:, b.slot, :, 1], var_eps[:, :],
                                   ALU.add).then_inc(variance_made, 1)
                pool.wait_ge(variance_made, b.at + 1)
                pool.tensor_tensor(inv_std[:, b.slot, :], variance[:, :], minus_half[:, :],
                                   ALU.pow).then_inc(inv_std_made, 1)
                pool.wait_ge(inv_std_made, b.at + 1)
                pool.tensor_tensor(shift[:, b.slot, :], neg_mean[:, :], inv_std[:, b.slot, :],
                                   ALU.mult).then_inc(shift_made, 1)

            def iteration(b, n=None):
                for t in range(NT):
                    low_g1(b, t)
                if n:
                    for j in range(NT):
                        low_alpha(n, j)
                norm_factors(b)

            pool.memset(minus_half[:, :], -0.5)
            pool.memset(minus_one[:, :], -1.0)
            pool.memset(var_eps[:, :], VAR_EPS)
            pool.memset(ident[:, :], 0.0).then_inc(ident_zeroed, 1)
            pool.wait_ge(ident_zeroed, 1)
            pool.affine_select(out=ident[:, :], in_=ident[:, :], compare_op=ALU.not_equal, fill=1.0,
                               base=0, pattern=[[-1, P]], channel_multiplier=1).then_inc(ident_made, 1)
            pool.memset(g2_high[:, :, D:D + 2].bitcast(F32), 1.0).then_inc(ones_made, 1)
            n = batch(0)
            for j in range(NT):
                low_alpha(n, j)
            iteration(batch(0), batch(1))
            iteration(batch(1), batch(2))
            with pool.Fori(1, B // 2 - 1) as i:
                for ahead in range(2):
                    iteration(in_loop(i, ahead), in_loop(i, ahead + 1))
            iteration(batch(B - 2), batch(B - 1))
            iteration(batch(B - 1))


_INS = ["x", "adj", "L0_gnn_Wv", "L0_gnn_bv", "L0_gnn_aw", "L0_gnn_ab", "L0_gnn_Wk", "L0_gnn_bk"]


def kernel(**inputs):
    import numpy as _np
    import concourse.bacc as _bacc
    from concourse import mybir as _mybir
    from concourse.bass_utils import run_bass_kernel_spmd as _run

    nc = _bacc.Bacc("TRN2", target_bir_lowering=False, num_devices=1)
    arrays, args = {}, []
    for name in _INS:
        a = _np.ascontiguousarray(inputs[name])
        arrays[f"in_{name}_dram"] = a
        args.append(nc.dram_tensor(f"in_{name}_dram", a.shape, _mybir.dt.from_np(a.dtype), kind="ExternalInput").ap())
    shape = arrays["in_x_dram"].shape
    args.append(nc.dram_tensor("out_0_dram", shape, _mybir.dt.float32, kind="ExternalOutput").ap())
    gnn_resnorm(nc, *args)
    r = _run(nc, [arrays], core_ids=[0])
    return r.results[0]["out_0_dram"]
```

```python
from collections import namedtuple
from contextlib import ExitStack

from concourse import mybir

ALU = mybir.AluOpType
ACT = mybir.ActivationFunctionType
F32 = mybir.dt.float32
F32R = mybir.dt.float32r

P = 128
SLOPE = 0.2
SUM_EPS = 1e-12
VAR_EPS = 1e-5
WARM_UPS_X = 12
WARM_UPS_W = 7

Batch = namedtuple("Batch", "at pair slot")


def batch(number):
    return Batch(number, number // 2, number % 2)


FIRST = batch(0)
SECOND = batch(1)


def in_loop(i, ahead):
    return Batch(2 * i + ahead, i + ahead // 2, ahead % 2)


def after(engine, semaphore, count):
    if not isinstance(count, int) or count > 0:
        engine.wait_ge(semaphore, count)


def gnn_resnorm(nc, x, adj, Wv, bv, aw, ab, Wk, bk, out):
    B, N, D = x.shape
    HOPS = Wk.shape[0]
    NT = N // P
    DT = D // P
    WA = 2 * D
    WB = D + 4
    SJ, SJ_REST, SI = D, D + 1, D + 2
    LAST = batch(B - 1)
    EARLY = NT // 2
    assert N == 4 * P and D == 2 * P and HOPS == 3 and B % 2 == 0

    with ExitStack() as ctx:
        def sb(name, shape, dt=F32):
            return ctx.enter_context(nc.sbuf_tensor(name, shape, dt))

        def psum(name, shape):
            return ctx.enter_context(nc.psum_tensor(name, shape, F32))

        def sem(name):
            return ctx.enter_context(nc.semaphore(name))

        hop_ps = psum("hop_ps", [P, 2, 512])
        feat_ps = psum("feat_ps", [P, 2, 512])
        adj_ps = psum("adj_ps", [P, 2, 512])
        xt_ps = psum("xt_ps", [P, 2, 512])

        ident = sb("ident", [P, P])
        minus_half = sb("minus_half", [P, NT])
        minus_one = sb("minus_one", [P, NT])
        var_eps = sb("var_eps", [P, NT])
        w_raw = sb("w_raw", [P, DT, WA + WB])
        w_high = sb("w_high", [P, DT, WA + WB], F32R)
        w_low = sb("w_low", [P, DT, WA + WB], F32R)
        wv_sb = sb("wv_sb", [P, DT, D])
        aw_row = sb("aw_row", [P, 2, D])
        bv_row = sb("bv_row", [P, D])
        bk_rows = sb("bk_rows", [HOPS, D])
        ones = sb("ones", [HOPS, P])
        ab_col = sb("ab_col", [P, 1])
        scratch = sb("scratch", [P, 6, D])
        dots = sb("dots", [P, 4])
        bias_row = sb("bias_row", [P, WB])

        x_in = sb("x_in", [P, 2, NT, D])
        x_res = sb("x_res", [P, 2, NT, D])
        a_in = sb("a_in", [P, 2, NT, N])
        xt_high = sb("xt_high", [P, DT, N], F32R)
        xt_low = sb("xt_low", [P, DT, N], F32R)
        xw0 = sb("xw0", [P, 2, NT, WB])
        xw1 = sb("xw1", [P, NT, D])
        g2_high = sb("g2_high", [P, NT, D + 2], F32R)
        g2_low = sb("g2_low", [P, NT, D], F32R)
        si_slope = sb("si_slope", [P, N])
        expo = sb("expo", [P, NT, N])
        alpha = sb("alpha", [P, NT, N])
        alpha_high = sb("alpha_high", [P, 2, NT, N], F32R)
        alpha_low = sb("alpha_low", [P, 2, NT, N], F32R)
        rowsum = sb("rowsum", [P, NT])
        inv_sum = sb("inv_sum", [P, NT])
        g1 = sb("g1", [P, NT, D])
        g1_high = sb("g1_high", [P, NT, D], F32R)
        g1_low = sb("g1_low", [P, NT, D], F32R)
        h = sb("h", [P, 2, D])
        y = sb("y", [P, 2, NT, D])
        stats = sb("stats", [P, NT, 6])
        moments = sb("moments", [P, 2, NT, 2])
        neg_mean = sb("neg_mean", [P, 2, NT])
        variance = sb("variance", [P, 2, NT])
        inv_std = sb("inv_std", [P, 2, NT])
        shift = sb("shift", [P, 2, NT])

        ident_zeroed = sem("ident_zeroed")
        ident_made = sem("ident_made")
        ones_made = sem("ones_made")
        wv_loaded = sem("wv_loaded")
        aw_loaded = sem("aw_loaded")
        w0_loaded = sem("w0_loaded")
        wa_loaded = sem("wa_loaded")
        bv_loaded = sem("bv_loaded")
        ab_loaded = sem("ab_loaded")
        bk_loaded = sem("bk_loaded")
        dots_made = sem("dots_made")
        bias_ones_made = sem("bias_ones_made")
        bias_summed = sem("bias_summed")
        bias_sum_kept = sem("bias_sum_kept")
        bias_dots_made = sem("bias_dots_made")
        bias_made = sem("bias_made")
        w0_high_made = sem("w0_high_made")
        w0_split = sem("w0_split")
        folded = sem("folded")
        folded_high_made = sem("folded_high_made")
        folded_split = sem("folded_split")
        wa_high_made = sem("wa_high_made")
        wa_split = sem("wa_split")
        x_loaded = [sem(f"x_loaded{s}") for s in range(2)]
        a_loaded = [sem(f"a_loaded{s}") for s in range(2)]
        stored = [sem(f"stored{s}") for s in range(2)]

        xt_turned = sem("xt_turned")
        featB_done = sem("featB_done")
        featA_done = sem("featA_done")
        si_spread = sem("si_spread")
        adj_turned = sem("adj_turned")
        hop1_done = sem("hop1_done")
        hop2_done = sem("hop2_done")

        xt_high_made = sem("xt_high_made")
        g2_high_made = sem("g2_high_made")
        si_sloped = sem("si_sloped")
        expo_done = sem("expo_done")
        alpha_high_made = sem("alpha_high_made")
        g1_high_made = sem("g1_high_made")
        normalised = sem("normalised")
        last_normalised = sem("last_normalised")

        xt_split = sem("xt_split")
        feat_out = [sem(f"feat_out{s}") for s in range(2)]
        hop_out = [sem(f"hop_out{s}") for s in range(2)]
        alpha_made = [sem(f"alpha_made{s}") for s in range(2)]
        scores_made = sem("scores_made")
        rowsum_made = sem("rowsum_made")
        inv_sum_made = sem("inv_sum_made")
        y_made = sem("y_made")
        stats_made = sem("stats_made")
        moments_made = sem("moments_made")
        variance_made = sem("variance_made")
        inv_std_made = sem("inv_std_made")
        neg_mean_made = sem("neg_mean_made")
        shift_made = sem("shift_made")

        res_kept = sem("res_kept")
        alpha_split = sem("alpha_split")
        g1_split = sem("g1_split")

        x_d = x.rearrange("b (t p) d -> b p t d", p=P)
        a_d = adj.rearrange("b (t p) j -> b p t j", p=P)
        out_d = out.rearrange("b (t p) d -> b p t d", p=P)
        wk_d = Wk.rearrange("k (t p) e -> k p t e", p=P)
        wv_d = Wv.rearrange("(t p) e -> p t e", p=P)

        def si_rows(n):
            return hop_ps[:, 1, :] if n is FIRST else xt_ps[:, 0, :]

        def hop2_bank(b, t):
            return feat_ps[:, t, 0:D] if b is LAST and t < 2 else hop_ps[:, t % 2, 0:D]

        bias_ps = adj_ps[:, 1, 0:D]

        block = ctx.enter_context(nc.Block())

        @block.sync
        def _(sp):
            def load_x(n):
                sp.dma_start(x_in[:, n.slot], x_d[n.at]).then_inc(x_loaded[n.slot], 16)

            def load_a(n):
                sp.dma_start(a_in[:, n.slot], a_d[n.at]).then_inc(a_loaded[n.slot], 16)

            def replace(n):
                m = Batch(n.at + 2, n.pair + 1, n.slot)
                sp.wait_ge(adj_turned, NT * (n.at + 1))
                load_a(m)
                sp.wait_ge(xt_turned, DT * (n.at + 1))
                sp.wait_ge(res_kept, n.at + 1)
                load_x(m)

            def store(b):
                sp.wait_ge(normalised, NT * (b.at + 1))
                sp.dma_start(out_d[b.at], y[:, b.slot]).then_inc(stored[b.slot], 16)

            load_x(batch(0))
            sp.dma_start(wv_sb[:, :, :], wv_d).then_inc(wv_loaded, 16)
            for c, k in enumerate((2, 1)):
                sp.dma_start(w_raw[:, :, c * D:(c + 1) * D], wk_d[k]).then_inc(wa_loaded, 16)
            load_a(batch(0))
            load_x(batch(1))
            load_a(batch(1))
            replace(batch(0))
            replace(batch(1))
            with sp.Fori(1, B // 2 - 1) as i:
                for ahead in range(2):
                    replace(in_loop(i, ahead))
                    store(in_loop(i, ahead - 2))
            for b in range(B - 4, B - 1):
                store(batch(b))
            sp.wait_ge(normalised, NT * LAST.at + EARLY)
            sp.dma_start(out_d[LAST.at][:, :EARLY], y[:, LAST.slot, :EARLY]).then_inc(stored[LAST.slot], 16)
            for t in range(EARLY, NT):
                sp.wait_ge(last_normalised, t - EARLY + 1)
                sp.dma_start(out_d[LAST.at][:, t], y[:, LAST.slot, t]).then_inc(stored[LAST.slot], 16)
            sp.wait_ge(stored[0], 16 * (B // 2))
            sp.wait_ge(stored[1], 16 * (B // 2 + NT - EARLY))

        @block.tensor
        def _(pe):
            def turn_x(m, dt):
                if dt == 0:
                    pe.wait_ge(x_loaded[m.slot], 16 * (m.pair + 1))
                    if m is not SECOND:
                        after(pe, scores_made, NT * m.at)
                else:
                    after(pe, xt_split, DT * m.at)
                for t in range(NT):
                    mm = pe.transpose(xt_ps[:, dt, t * P:(t + 1) * P],
                                      x_in[:, m.slot, t, dt * P:(dt + 1) * P], ident[:, :])
                mm.then_inc(xt_turned, 1)

            def split_product(ps, c0, c1, n, t):
                for dt in range(DT):
                    if t == 0:
                        pe.wait_ge(xt_split, DT * n.at + dt + 1)
                    xh = xt_high[:, dt, t * P:(t + 1) * P]
                    xl = xt_low[:, dt, t * P:(t + 1) * P]
                    pe.matmul(ps, xh, w_high[:, dt, c0:c1], start=(dt == 0), stop=False)
                    pe.matmul(ps, xh, w_low[:, dt, c0:c1], start=False, stop=False)
                    mm = pe.matmul(ps, xl, w_high[:, dt, c0:c1], start=False, stop=(dt == DT - 1))
                return mm

            def features_b(n, t):
                after(pe, feat_out[t % 2], 4 * n.at + t // 2)
                split_product(feat_ps[:, t % 2, 0:WB], WA, WA + WB, n, t).then_inc(featB_done, 1)

            def features_a(n, t):
                pe.wait_ge(feat_out[t % 2], 4 * n.at + 2 + t // 2)
                split_product(feat_ps[:, t % 2, 0:WA], 0, WA, n, t).then_inc(featA_done, 1)

            def spread_si(n):
                pe.wait_ge(feat_out[0], 4 * n.at + 2)
                pe.wait_ge(feat_out[1], 4 * n.at + 2)
                for t in range(NT):
                    mm = pe.transpose(si_rows(n)[:, t * P:(t + 1) * P],
                                      xw0[:, n.slot, t, SI:SI + 1].to_broadcast([P, P]), ident[:, :])
                mm.then_inc(si_spread, 1)

            def turn_adj(n, j):
                if j == 0:
                    pe.wait_ge(a_loaded[n.slot], 16 * (n.pair + 1))
                after(pe, alpha_made[j % 2], 2 * n.at + j // 2)
                for t in range(NT):
                    mm = pe.transpose(adj_ps[:, j % 2, t * P:(t + 1) * P],
                                      a_in[:, n.slot, t, j * P:(j + 1) * P], ident[:, :])
                mm.then_inc(adj_turned, 1)

            def hop1(b, t):
                if t == 0:
                    pe.wait_ge(feat_out[0], 4 * (b.at + 1))
                    pe.wait_ge(feat_out[1], 4 * (b.at + 1))
                after(pe, hop_out[t % 2], 4 * b.at + t // 2)
                ps = hop_ps[:, t % 2, :]
                for j in range(NT):
                    if t == 0:
                        pe.wait_ge(alpha_split, NT * b.at + j + 1)
                    ah = alpha_high[:, b.slot, j, t * P:(t + 1) * P]
                    al = alpha_low[:, b.slot, j, t * P:(t + 1) * P]
                    pe.matmul(ps[:, 0:D + 2], ah, g2_high[:, j, :], start=(j == 0), stop=False)
                    pe.matmul(ps[:, 0:D], ah, g2_low[:, j, :], start=False, stop=False)
                    mm = pe.matmul(ps[:, 0:D + 2], al, g2_high[:, j, :], start=False, stop=(j == NT - 1))
                mm.then_inc(hop1_done, 1)

            def hop2(b, t, sources=range(NT)):
                if b is not LAST:
                    pe.wait_ge(hop_out[t % 2], 4 * b.at + 2 + t // 2)
                elif t >= 2:
                    pe.wait_ge(hop_out[t % 2], 4 * b.at + 2)
                ps = hop2_bank(b, t)
                for j in sources:
                    if t == 0:
                        pe.wait_ge(g1_high_made, NT * b.at + j + 1)
                    ah = alpha_high[:, b.slot, j, t * P:(t + 1) * P]
                    al = alpha_low[:, b.slot, j, t * P:(t + 1) * P]
                    pe.matmul(ps, ah, g1_high[:, j, :], start=(j == 0), stop=False)
                    pe.matmul(ps, al, g1_high[:, j, :], start=False, stop=False)
                    if t == 0:
                        pe.wait_ge(g1_split, NT * b.at + j + 1)
                    mm = pe.matmul(ps, ah, g1_low[:, j, :], start=False, stop=(j == NT - 1))
                if NT - 1 in sources:
                    mm.then_inc(hop2_done, 1)

            def sum_bias():
                pe.wait_ge(bias_ones_made, 1)
                pe.wait_ge(bk_loaded, 16)
                pe.matmul(bias_ps, ones[:, :], bk_rows[:, :], start=True, stop=True).then_inc(bias_summed, 1)

            def warm_up(transposes):
                for _ in range(transposes):
                    pe.transpose(adj_ps[:, 0, 0:P], ident[:, :], ident[:, :])

            def iteration(b, n=None, m=None):
                hop1(b, 0)
                hop1(b, 1)
                if n:
                    spread_si(n)
                hop1(b, 2)
                hop1(b, 3)
                if n:
                    for t in range(NT - 1):
                        features_a(n, t)
                        turn_adj(n, t)
                    features_a(n, NT - 1)
                if m:
                    turn_x(m, 0)
                    turn_x(m, 1)
                if n:
                    turn_adj(n, NT - 1)
                if b is LAST:
                    for sources in (range(NT // 2), range(NT // 2, NT)):
                        hop2(b, 0, sources)
                        hop2(b, 1, sources)
                for t in range(2 if b is LAST else 0, NT):
                    hop2(b, t)
                    if m:
                        features_b(m, t)

            pe.wait_ge(ident_made, 1)
            warm_up(WARM_UPS_X)
            turn_x(FIRST, 0)
            turn_x(FIRST, 1)
            sum_bias()
            warm_up(WARM_UPS_W)
            pe.wait_ge(w0_split, 1)
            pe.wait_ge(folded_split, 1)
            for t in range(NT):
                features_b(FIRST, t)
            spread_si(FIRST)
            pe.wait_ge(wa_split, 1)
            features_a(FIRST, 0)
            features_a(FIRST, 1)
            turn_adj(FIRST, 0)
            features_a(FIRST, 2)
            turn_adj(FIRST, 1)
            features_a(FIRST, 3)
            turn_x(SECOND, 0)
            turn_x(SECOND, 1)
            turn_adj(FIRST, 2)
            turn_adj(FIRST, 3)
            features_b(SECOND, 0)
            features_b(SECOND, 1)
            features_b(SECOND, 2)
            features_b(SECOND, 3)
            pe.wait_ge(ones_made, 1)
            iteration(batch(0), batch(1), batch(2))
            iteration(batch(1), batch(2), batch(3))
            with pe.Fori(1, B // 2 - 1) as i:
                for ahead in range(2):
                    iteration(in_loop(i, ahead), in_loop(i, ahead + 1), in_loop(i, ahead + 2))
            iteration(batch(B - 2), batch(B - 1))
            iteration(LAST)

        @block.scalar
        def _(act):
            def high_x(m, dt):
                act.wait_ge(xt_turned, DT * m.at + dt + 1)
                act.copy(xt_high[:, dt, :], xt_ps[:, dt, :]).then_inc(xt_high_made, 1)

            def high_g2(n, t):
                act.wait_ge(featA_done, NT * n.at + t + 1)
                act.copy(g2_high[:, t, 0:D], feat_ps[:, t % 2, 0:D])
                act.copy(xw1[:, t, :], feat_ps[:, t % 2, D:2 * D]).then_inc(g2_high_made, 1)

            def slope_si(n):
                act.wait_ge(si_spread, n.at + 1)
                act.mul(si_slope[:, :], si_rows(n), SLOPE).then_inc(si_sloped, 1)

            def exponential(n, j):
                act.wait_ge(scores_made, NT * n.at + j + 1)
                act.activation(expo[:, j, :], expo[:, j, :], ACT.Exp,
                               bias=xw0[:, n.slot, j, SJ:SJ + 1]).then_inc(expo_done, 1)

            def high_alpha(n, j):
                act.wait_ge(alpha_made[j % 2], 2 * n.at + j // 2 + 1)
                act.copy(alpha_high[:, n.slot, j, :], alpha[:, j, :]).then_inc(alpha_high_made, 1)

            def high_g1(b, t):
                if t == 0:
                    after(act, hop2_done, NT * b.at)
                act.wait_ge(hop_out[t % 2], 4 * b.at + t // 2 + 1)
                act.copy(g1_high[:, t, :], g1[:, t, :]).then_inc(g1_high_made, 1)

            def normalise(b, tiles=range(NT)):
                act.wait_ge(shift_made, b.at + 1)
                for t in tiles:
                    act.activation(y[:, b.slot, t, :], y[:, b.slot, t, :], ACT.Identity,
                                   bias=shift[:, b.slot, t:t + 1],
                                   scale=inv_std[:, b.slot, t:t + 1]).then_inc(normalised, 1)

            def keep_residual(n):
                act.wait_ge(x_loaded[n.slot], 16 * (n.pair + 1))
                after(act, y_made, NT * (n.at - 1))
                act.copy(x_res[:, n.slot], x_in[:, n.slot]).then_inc(res_kept, 1)

            def iteration(b, n=None, m=None, last=None):
                high_g1(b, 0)
                if n:
                    slope_si(n)
                high_g1(b, 1)
                if n:
                    exponential(n, 0)
                high_g1(b, 2)
                if n:
                    exponential(n, 1)
                high_g1(b, 3)
                if n:
                    high_g2(n, 0)
                    exponential(n, 2)
                    high_g2(n, 1)
                    exponential(n, 3)
                    high_alpha(n, 0)
                    high_g2(n, 2)
                    high_alpha(n, 1)
                    high_g2(n, 3)
                if m:
                    high_x(m, 0)
                    high_x(m, 1)
                if n:
                    high_alpha(n, NT - 2)
                    high_alpha(n, NT - 1)
                    keep_residual(n)
                if last:
                    normalise(last)

            act.dma_start(aw_row[:, :, :].rearrange("p m e -> p (m e)"),
                          aw.rearrange("e o -> (o e)").partition_broadcast(P)).then_inc(aw_loaded, 16)
            act.dma_start(w_raw[:, :, WA:WA + D], wk_d[0]).then_inc(w0_loaded, 16)
            act.dma_start(ab_col[:, :], ab.partition_broadcast(P)).then_inc(ab_loaded, 16)
            act.preload_act_table(ACT.Exp)
            high_x(FIRST, 0)
            act.wait_ge(w0_loaded, 16)
            act.copy(w_high[:, :, WA:WA + D], w_raw[:, :, WA:WA + D]).then_inc(w0_high_made, 1)
            high_x(FIRST, 1)
            act.wait_ge(folded, 1)
            act.copy(w_high[:, :, WA + D:], w_raw[:, :, WA + D:]).then_inc(folded_high_made, 1)
            act.wait_ge(bias_summed, 1)
            act.copy(bias_row[:, 0:D], bias_ps).then_inc(bias_sum_kept, 1)
            act.wait_ge(wa_loaded, 2 * 16)
            act.copy(w_high[:, :, 0:WA], w_raw[:, :, 0:WA]).then_inc(wa_high_made, 1)
            keep_residual(FIRST)
            slope_si(FIRST)
            high_g2(FIRST, 0)
            exponential(FIRST, 0)
            exponential(FIRST, 1)
            high_g2(FIRST, 1)
            exponential(FIRST, 2)
            exponential(FIRST, 3)
            high_g2(FIRST, 2)
            high_alpha(FIRST, 0)
            high_g2(FIRST, 3)
            high_x(SECOND, 0)
            high_x(SECOND, 1)
            high_alpha(FIRST, 1)
            high_alpha(FIRST, 2)
            high_alpha(FIRST, 3)
            iteration(batch(0), batch(1), batch(2))
            iteration(batch(1), batch(2), batch(3), batch(0))
            with act.Fori(1, B // 2 - 1) as i:
                for ahead in range(2):
                    iteration(in_loop(i, ahead), in_loop(i, ahead + 1), in_loop(i, ahead + 2),
                              in_loop(i, ahead - 1))
            iteration(batch(B - 2), batch(B - 1), None, batch(B - 3))
            iteration(LAST, None, None, batch(B - 2))
            normalise(LAST, range(EARLY))

        @block.vector
        def _(dve):
            def low_x(m, dt):
                dve.wait_ge(xt_high_made, DT * m.at + dt + 1)
                dve.tensor_tensor(xt_low[:, dt, :], xt_ps[:, dt, :], xt_high[:, dt, :].bitcast(F32),
                                  ALU.subtract).then_inc(xt_split, 1)

            def keep_xw0(n, t):
                dve.wait_ge(featB_done, NT * n.at + t + 1)
                dve.tensor_tensor(xw0[:, n.slot, t, :], feat_ps[:, t % 2, 0:WB], bias_row[:, :],
                                  ALU.add).then_inc(feat_out[t % 2], 1)

            def low_g2(n, t):
                dve.wait_ge(g2_high_made, NT * n.at + t + 1)
                dve.tensor_tensor(g2_low[:, t, :], feat_ps[:, t % 2, 0:D], g2_high[:, t, 0:D].bitcast(F32),
                                  ALU.subtract).then_inc(feat_out[t % 2], 1)

            def score(n, j):
                if j == 0:
                    dve.wait_ge(si_sloped, n.at + 1)
                    after(dve, alpha_made[0], 2 * n.at)
                    after(dve, alpha_made[1], 2 * n.at)
                dve.scalar_tensor_tensor(out=expo[:, j, :], in0=si_slope[:, :],
                                         scalar=xw0[:, n.slot, j, SJ_REST:SJ_REST + 1],
                                         in1=si_rows(n), op0=ALU.add,
                                         op1=ALU.max).then_inc(scores_made, 1)

            def make_alpha(n, j):
                if j == 0:
                    after(dve, alpha_split, NT * n.at)
                dve.wait_ge(adj_turned, NT * n.at + j + 1)
                dve.wait_ge(expo_done, NT * n.at + j + 1)
                dve.tensor_tensor(alpha[:, j, :], adj_ps[:, j % 2, :], expo[:, j, :],
                                  ALU.mult).then_inc(alpha_made[j % 2], 1)

            def low_alpha(n, j):
                dve.wait_ge(alpha_high_made, NT * n.at + j + 1)
                dve.tensor_tensor(alpha_low[:, n.slot, j, :], alpha[:, j, :],
                                  alpha_high[:, n.slot, j, :].bitcast(F32),
                                  ALU.subtract).then_inc(alpha_split, 1)

            def leave_hop1(b, t):
                if t == 0:
                    after(dve, g1_split, NT * b.at)
                dve.wait_ge(hop1_done, NT * b.at + t + 1)
                dve.tensor_scalar(rowsum[:, t:t + 1], hop_ps[:, t % 2, D:D + 1], SUM_EPS, None,
                                  ALU.add).then_inc(rowsum_made, 1)
                dve.wait_ge(rowsum_made, NT * b.at + t + 1)
                dve.reciprocal(inv_sum[:, t:t + 1], rowsum[:, t:t + 1]).then_inc(inv_sum_made, 1)
                dve.wait_ge(inv_sum_made, NT * b.at + t + 1)
                dve.scalar_tensor_tensor(out=g1[:, t, :], in0=hop_ps[:, t % 2, 0:D],
                                         scalar=inv_sum[:, t:t + 1], in1=xw1[:, t, :],
                                         op0=ALU.mult, op1=ALU.add).then_inc(hop_out[t % 2], 1)

            def low_g1(b, t):
                dve.wait_ge(g1_high_made, NT * b.at + t + 1)
                dve.tensor_tensor(g1_low[:, t, :], g1[:, t, :], g1_high[:, t, :].bitcast(F32),
                                  ALU.subtract).then_inc(g1_split, 1)

            def leave_hop2(b, t):
                dve.wait_ge(hop2_done, NT * b.at + t + 1)
                dve.scalar_tensor_tensor(out=h[:, t % 2, :], in0=hop2_bank(b, t),
                                         scalar=inv_sum[:, t:t + 1], in1=xw0[:, b.slot, t, 0:D],
                                         op0=ALU.mult, op1=ALU.add).then_inc(hop_out[t % 2], 1)

            def add_residual(b, t):
                if t == 0:
                    after(dve, stored[b.slot], 16 * b.pair)
                    dve.wait_ge(res_kept, b.at + 1)
                dve.wait_ge(hop_out[t % 2], 4 * b.at + 2 + t // 2 + 1)
                dve.scalar_tensor_tensor(out=y[:, b.slot, t, :], in0=h[:, t % 2, :], scalar=0.0,
                                         in1=x_res[:, b.slot, t, :], op0=ALU.max,
                                         op1=ALU.add).then_inc(y_made, 1)

            def measure(b, t):
                dve.wait_ge(y_made, NT * b.at + t + 1)
                dve.bn_stats(stats[:, t, :], y[:, b.slot, t, :]).then_inc(stats_made, 1)

            def gather_moments(b, tiles=range(NT)):
                for t in tiles:
                    last = dve.bn_aggr(moments[:, b.slot, t, :], stats[:, t, :])
                last.then_inc(moments_made, 1)

            def iteration(b, n=None, m=None):
                leave_hop1(b, 0)
                if b is LAST:
                    measure(batch(B - 2), NT - 1)
                leave_hop1(b, 1)
                if n:
                    score(n, 0)
                if b is LAST:
                    low_g1(b, 0)
                    dve.wait_ge(stats_made, NT * b.at)
                    gather_moments(batch(B - 2))
                leave_hop1(b, 2)
                if n:
                    score(n, 1)
                if b is LAST:
                    low_g1(b, 1)
                leave_hop1(b, 3)
                if b is LAST:
                    low_g1(b, 2)
                    low_g1(b, 3)
                if n:
                    score(n, 2)
                    low_g2(n, 0)
                    score(n, 3)
                    make_alpha(n, 0)
                    low_g2(n, 1)
                    make_alpha(n, 1)
                    low_g2(n, 2)
                    make_alpha(n, 2)
                    low_g2(n, 3)
                if m:
                    low_x(m, 0)
                    low_x(m, 1)
                if n:
                    make_alpha(n, NT - 1)
                if b is LAST:
                    return
                for t in range(NT):
                    leave_hop2(b, t)
                    add_residual(b, t)
                    if t == NT - 1 and n and not m:
                        return
                    measure(b, t)
                    if t == NT - 1:
                        dve.wait_ge(stats_made, NT * (b.at + 1))
                    if m:
                        keep_xw0(m, t)
                gather_moments(b)

            def finish_last():
                leave_hop2(LAST, 0)
                add_residual(LAST, 0)
                leave_hop2(LAST, 1)
                measure(LAST, 0)
                add_residual(LAST, 1)
                leave_hop2(LAST, 2)
                measure(LAST, 1)
                add_residual(LAST, 2)
                dve.wait_ge(stats_made, NT * LAST.at + EARLY)
                gather_moments(LAST, range(EARLY))
                measure(LAST, 2)
                leave_hop2(LAST, 3)
                add_residual(LAST, 3)
                measure(LAST, 3)
                dve.wait_ge(stats_made, NT * B)
                gather_moments(LAST, range(EARLY, NT))
                dve.wait_ge(inv_std_made, LAST.at + 2)
                for t in range(EARLY, NT):
                    dve.tensor_scalar(y[:, LAST.slot, t, :], y[:, LAST.slot, t, :],
                                      moments[:, LAST.slot, t, 0:1], inv_std[:, LAST.slot, t:t + 1],
                                      ALU.subtract, ALU.mult).then_inc(last_normalised, 1)

            dve.memset(ones[:, :], 1.0).then_inc(bias_ones_made, 1)
            dve.memset(bias_row[:, SI:WB], 0.0)
            dve.memset(w_raw[:, :, WA + SI + 1:WA + WB], 0.0)
            dve.wait_ge(wv_loaded, 16)
            dve.wait_ge(aw_loaded, 16)
            for half, column in enumerate((WA + SJ, WA + SI)):
                for dt in range(DT):
                    dve.tensor_tensor_reduce(scratch[:, 2 * half + dt, :], wv_sb[:, dt, :], aw_row[:, half, :],
                                             1.0, 0.0, ALU.mult, ALU.add,
                                             w_raw[:, dt, column:column + 1]).then_inc(dots_made, 1)
            dve.wait_ge(dots_made, 2 * DT)
            dve.tensor_scalar(w_raw[:, :, WA + SJ_REST], w_raw[:, :, WA + SJ], SLOPE - 1.0, None,
                              ALU.mult).then_inc(folded, 1)
            low_x(FIRST, 0)
            low_x(FIRST, 1)
            dve.wait_ge(folded_high_made, 1)
            dve.tensor_tensor(w_low[:, :, WA + D:], w_raw[:, :, WA + D:], w_high[:, :, WA + D:].bitcast(F32),
                              ALU.subtract).then_inc(folded_split, 1)
            dve.wait_ge(bv_loaded, 16)
            for half in range(2):
                dve.tensor_tensor_reduce(scratch[:, 4 + half, :], bv_row[:, :], aw_row[:, half, :],
                                         1.0, 0.0, ALU.mult, ALU.add,
                                         dots[:, half:half + 1]).then_inc(bias_dots_made, 1)
            dve.wait_ge(bias_dots_made, 2)
            dve.tensor_tensor(dots[:, 2:3], dots[:, 0:1], dots[:, 1:2], ALU.add).then_inc(bias_dots_made, 1)
            dve.wait_ge(bias_dots_made, 3)
            dve.wait_ge(ab_loaded, 16)
            dve.tensor_tensor(bias_row[:, SJ:SJ + 1], dots[:, 2:3], ab_col[:, :], ALU.add).then_inc(bias_made, 1)
            dve.wait_ge(bias_made, 1)
            dve.tensor_scalar(bias_row[:, SJ_REST:SJ_REST + 1], bias_row[:, SJ:SJ + 1], SLOPE - 1.0, None,
                              ALU.mult).then_inc(bias_made, 1)
            dve.wait_ge(bias_made, 2)
            dve.wait_ge(bias_sum_kept, 1)
            for t in range(NT):
                keep_xw0(FIRST, t)
            score(FIRST, 0)
            score(FIRST, 1)
            low_g2(FIRST, 0)
            score(FIRST, 2)
            score(FIRST, 3)
            low_g2(FIRST, 1)
            make_alpha(FIRST, 0)
            low_g2(FIRST, 2)
            make_alpha(FIRST, 1)
            low_g2(FIRST, 3)
            low_x(SECOND, 0)
            low_x(SECOND, 1)
            make_alpha(FIRST, 2)
            keep_xw0(SECOND, 0)
            make_alpha(FIRST, 3)
            keep_xw0(SECOND, 1)
            dve.wait_ge(alpha_split, NT - 1)
            low_alpha(FIRST, NT - 1)
            keep_xw0(SECOND, 2)
            keep_xw0(SECOND, 3)
            iteration(batch(0), batch(1), batch(2))
            iteration(batch(1), batch(2), batch(3))
            with dve.Fori(1, B // 2 - 1) as i:
                for ahead in range(2):
                    iteration(in_loop(i, ahead), in_loop(i, ahead + 1), in_loop(i, ahead + 2))
            iteration(batch(B - 2), batch(B - 1))
            iteration(LAST)
            finish_last()

        @block.gpsimd
        def _(pool):
            def low_g1(b, t):
                pool.wait_ge(g1_high_made, NT * b.at + t + 1)
                pool.tensor_tensor(g1_low[:, t, :], g1[:, t, :], g1_high[:, t, :].bitcast(F32),
                                   ALU.subtract).then_inc(g1_split, 1)

            def low_alpha(n, j):
                pool.wait_ge(alpha_high_made, NT * n.at + j + 1)
                pool.tensor_tensor(alpha_low[:, n.slot, j, :], alpha[:, j, :],
                                   alpha_high[:, n.slot, j, :].bitcast(F32),
                                   ALU.subtract).then_inc(alpha_split, 1)

            def inverse_std(b, part=0, tiles=slice(0, NT)):
                pool.wait_ge(moments_made, b.at + part + 1)
                pool.tensor_tensor(variance[:, b.slot, tiles], moments[:, b.slot, tiles, 1], var_eps[:, tiles],
                                   ALU.add).then_inc(variance_made, 1)
                pool.wait_ge(variance_made, b.at + part + 1)
                pool.tensor_tensor(inv_std[:, b.slot, tiles], variance[:, b.slot, tiles], minus_half[:, tiles],
                                   ALU.pow).then_inc(inv_std_made, 1)

            def mean_shift(b, tiles=slice(0, NT)):
                pool.tensor_tensor(neg_mean[:, b.slot, tiles], moments[:, b.slot, tiles, 0], minus_one[:, tiles],
                                   ALU.mult).then_inc(neg_mean_made, 1)
                pool.wait_ge(inv_std_made, b.at + 1)
                pool.wait_ge(neg_mean_made, b.at + 1)
                pool.tensor_tensor(shift[:, b.slot, tiles], neg_mean[:, b.slot, tiles], inv_std[:, b.slot, tiles],
                                   ALU.mult).then_inc(shift_made, 1)

            def iteration(b, n=None):
                if b is not LAST:
                    for t in range(NT):
                        low_g1(b, t)
                if n:
                    for j in range(NT):
                        low_alpha(n, j)
                if b is LAST:
                    inverse_std(b, 0, slice(0, EARLY))
                    mean_shift(b, slice(0, EARLY))
                    inverse_std(b, 1, slice(EARLY, NT))
                else:
                    inverse_std(b)
                    mean_shift(b)

            pool.memset(ident[:, :], 0.0).then_inc(ident_zeroed, 1)
            pool.wait_ge(ident_zeroed, 1)
            pool.affine_select(out=ident[:, :], in_=ident[:, :], compare_op=ALU.not_equal, fill=1.0,
                               base=0, pattern=[[-1, P]], channel_multiplier=1).then_inc(ident_made, 1)
            pool.memset(g2_high[:, :, D:D + 2].bitcast(F32), 1.0).then_inc(ones_made, 1)
            pool.memset(minus_half[:, :], -0.5)
            pool.memset(minus_one[:, :], -1.0)
            pool.memset(var_eps[:, :], VAR_EPS)
            pool.dma_start(bk_rows[:, :], bk).then_inc(bk_loaded, 16)
            pool.dma_start(bv_row[:, :], bv.partition_broadcast(P)).then_inc(bv_loaded, 16)
            pool.wait_ge(w0_high_made, 1)
            pool.tensor_tensor(w_low[:, :, WA:WA + D], w_raw[:, :, WA:WA + D], w_high[:, :, WA:WA + D].bitcast(F32),
                               ALU.subtract).then_inc(w0_split, 1)
            pool.wait_ge(wa_high_made, 1)
            pool.tensor_tensor(w_low[:, :, 0:WA], w_raw[:, :, 0:WA], w_high[:, :, 0:WA].bitcast(F32),
                               ALU.subtract).then_inc(wa_split, 1)
            for j in range(NT - 1):
                low_alpha(FIRST, j)
            iteration(batch(0), batch(1))
            iteration(batch(1), batch(2))
            with pool.Fori(1, B // 2 - 1) as i:
                for ahead in range(2):
                    iteration(in_loop(i, ahead), in_loop(i, ahead + 1))
            iteration(batch(B - 2), batch(B - 1))
            iteration(LAST)


_INS = ["x", "adj", "L0_gnn_Wv", "L0_gnn_bv", "L0_gnn_aw", "L0_gnn_ab", "L0_gnn_Wk", "L0_gnn_bk"]


def kernel(**inputs):
    import numpy as _np
    import concourse.bacc as _bacc
    from concourse import mybir as _mybir
    from concourse.bass_utils import run_bass_kernel_spmd as _run

    nc = _bacc.Bacc("TRN2", target_bir_lowering=False, num_devices=1)
    arrays, args = {}, []
    for name in _INS:
        a = _np.ascontiguousarray(inputs[name])
        arrays[f"in_{name}_dram"] = a
        args.append(nc.dram_tensor(f"in_{name}_dram", a.shape, _mybir.dt.from_np(a.dtype), kind="ExternalInput").ap())
    shape = arrays["in_x_dram"].shape
    args.append(nc.dram_tensor("out_0_dram", shape, _mybir.dt.float32, kind="ExternalOutput").ap())
    gnn_resnorm(nc, *args)
    r = _run(nc, [arrays], core_ids=[0])
    return r.results[0]["out_0_dram"]
```
